# Optimizing a Trainium2 kernel written in Bass

```python
import numpy as np
import jax
import jax.numpy as jnp

def _softmax(x, axis=-1):
    return jax.nn.softmax(x, axis=axis)

def _gelu(x):
    return jax.nn.gelu(x, approximate=True)

def _silu(x):
    return jax.nn.silu(x)

def _sigmoid(x):
    return jax.nn.sigmoid(x)

def _layernorm(x, axis=-1, eps=1e-05):
    m = jnp.mean(x, axis=axis, keepdims=True)
    v = jnp.var(x, axis=axis, keepdims=True)
    return (x - m) / jnp.sqrt(v + eps)

def _scatter_add(tgt, idx, src, axis=0):
    return tgt.at[idx].add(src)

def _segment_sum(src, seg, n):
    return jax.ops.segment_sum(src, seg, n)
kernel_name = 'mk_cond_resid_d2_seqx_r4_b6b077'

def setup_inputs(seed: int=0):
    np.random.seed(seed)
    _w = jnp.asarray

    def _rec_inputs():
        import jax
        import jax.numpy as jnp
        _rk = jax.random.key(seed)
        x = -0.0003929 + 0.9999 * jax.random.normal(jax.random.fold_in(_rk, 1), (2, 1024, 256), jnp.float32)
        _lenS = 1024 - jax.random.randint(jax.random.fold_in(_rk, 7), (2,), 0, max(1, 1024 // 4) + 1, jnp.int32)
        _lenS2 = 1024 - jax.random.randint(jax.random.fold_in(_rk, 8), (2,), 0, max(1, 1024 // 4) + 1, jnp.int32)
        cond_1024 = 0.00386106 + 1.00199 * jax.random.normal(jax.random.fold_in(_rk, 11), (2, 256), jnp.float32)
        return (x, cond_1024)
    x, cond_1024 = _rec_inputs()

    def _L0_cond_setup():
        import jax, jax.numpy as jnp
        import numpy as np
        RANK = 8
        LN_EPS = 1e-05
        key = jax.random.key(seed)
        ks = jax.random.split(key, 8)
        B, T, D = (16, 256, 256)
        A = 256
        I = 256
        OUT = D * RANK * 4
        s = 0.02
        return {'x': jax.random.normal(ks[0], (B, T, D), jnp.float32), 'ada_emb': jax.random.normal(ks[1], (B, A), jnp.float32), 'base_up': jax.random.normal(ks[2], (D, D), jnp.float32) * s, 'base_down': jax.random.normal(ks[3], (D, D), jnp.float32) * s, 'ln_gamma': jnp.ones((A,), jnp.float32), 'ln_beta': jnp.zeros((A,), jnp.float32), 'W1': jax.random.normal(ks[4], (A, I), jnp.float32) / np.sqrt(A), 'bias1': jnp.zeros((I,), jnp.float32), 'W2': jax.random.normal(ks[5], (I, OUT), jnp.float32) / np.sqrt(I), 'bias2': jnp.zeros((OUT,), jnp.float32)}
    _L0_cond_all = _L0_cond_setup()
    _L0_cond_in = {k: v for k, v in _L0_cond_all.items() if k in ('base_up', 'base_down', 'ln_gamma', 'ln_beta', 'W1', 'bias1', 'W2', 'bias2')}
    del _L0_cond_all

    def _L1_cond_setup():
        import jax, jax.numpy as jnp
        import numpy as np
        NUM_EXPERTS = 4
        TOP_K = 2
        key = jax.random.key(seed)
        ks = jax.random.split(key, 16)
        B, L, D, E, H = (8, 192, 256, NUM_EXPERTS, 1024)
        s = 0.02
        return {'context_c': jax.random.normal(ks[0], (B, L, D), jnp.float32), 'time_cond': jax.random.normal(ks[1], (B, D), jnp.float32), 'gate_w': jax.random.normal(ks[2], (3 * D, E), jnp.float32) * s, 'gate_b': jnp.zeros((E,), jnp.float32), 'time_w': jax.random.normal(ks[3], (D, 2 * E), jnp.float32) * s, 'time_b': jnp.zeros((2 * E,), jnp.float32), 'ew1': jax.random.normal(ks[4], (E, D, H), jnp.float32) * s, 'eb1': jnp.zeros((E, H), jnp.float32), 'ew2': jax.random.normal(ks[5], (E, H, D), jnp.float32) * s, 'eb2': jnp.zeros((E, D), jnp.float32), 'sw1': jax.random.normal(ks[6], (D, H), jnp.float32) * s, 'sb1': jnp.zeros((H,), jnp.float32), 'sw2': jax.random.normal(ks[7], (H, D), jnp.float32) * s, 'sb2': jnp.zeros((D,), jnp.float32)}
    _L1_cond_all = _L1_cond_setup()
    _L1_cond_in = {k: v for k, v in _L1_cond_all.items() if k in ('gate_w', 'gate_b', 'time_w', 'time_b', 'ew1', 'eb1', 'ew2', 'eb2', 'sw1', 'sb1', 'sw2', 'sb2')}
    del _L1_cond_all
    return {'x': x, 'cond_1024': cond_1024, 'L0_cond_base_up': _L0_cond_in['base_up'], 'L0_cond_base_down': _L0_cond_in['base_down'], 'L0_cond_ln_gamma': _L0_cond_in['ln_gamma'], 'L0_cond_ln_beta': _L0_cond_in['ln_beta'], 'L0_cond_W1': _L0_cond_in['W1'], 'L0_cond_bias1': _L0_cond_in['bias1'], 'L0_cond_W2': _L0_cond_in['W2'], 'L0_cond_bias2': _L0_cond_in['bias2'], 'L1_cond_gate_w': _L1_cond_in['gate_w'], 'L1_cond_gate_b': _L1_cond_in['gate_b'], 'L1_cond_time_w': _L1_cond_in['time_w'], 'L1_cond_time_b': _L1_cond_in['time_b'], 'L1_cond_ew1': _L1_cond_in['ew1'], 'L1_cond_eb1': _L1_cond_in['eb1'], 'L1_cond_ew2': _L1_cond_in['ew2'], 'L1_cond_eb2': _L1_cond_in['eb2'], 'L1_cond_sw1': _L1_cond_in['sw1'], 'L1_cond_sb1': _L1_cond_in['sb1'], 'L1_cond_sw2': _L1_cond_in['sw2'], 'L1_cond_sb2': _L1_cond_in['sb2']}

def reference(x, cond_1024, L0_cond_base_up, L0_cond_base_down, L0_cond_ln_gamma, L0_cond_ln_beta, L0_cond_W1, L0_cond_bias1, L0_cond_W2, L0_cond_bias2, L1_cond_gate_w, L1_cond_gate_b, L1_cond_time_w, L1_cond_time_b, L1_cond_ew1, L1_cond_eb1, L1_cond_ew2, L1_cond_eb2, L1_cond_sw1, L1_cond_sb1, L1_cond_sw2, L1_cond_sb2):
    import jax
    import jax.numpy as jnp

    def _L0_cond_ref(x, ada_emb, base_up, base_down, ln_gamma, ln_beta, W1, bias1, W2, bias2):
        import jax, jax.numpy as jnp
        import numpy as np
        RANK = 8
        LN_EPS = 1e-05
        B, T, D = x.shape
        R = RANK
        mu = jnp.mean(ada_emb, axis=-1, keepdims=True)
        var = jnp.mean(jnp.square(ada_emb - mu), axis=-1, keepdims=True)
        c = (ada_emb - mu) / jnp.sqrt(var + LN_EPS) * ln_gamma + ln_beta
        h = jax.nn.gelu(c @ W1 + bias1, approximate=False)
        w = h @ W2 + bias2
        a1, b1, a2, b2 = [t.reshape(B, D, R) for t in jnp.split(w, 4, axis=-1)]
        u = jnp.einsum('btd,bdr->btr', x, a2)
        mid = jnp.einsum('btd,dl->btl', x, base_down) + jnp.einsum('btr,blr->btl', u, b2)
        mid = jax.nn.gelu(mid, approximate=False)
        v = jnp.einsum('blr,btl->btr', b1, mid)
        out = jnp.einsum('btl,kl->btk', mid, base_up) + jnp.einsum('bkr,btr->btk', a1, v)
        return x + out

    def _L1_cond_ref(context_c, time_cond, gate_w, gate_b, time_w, time_b, ew1, eb1, ew2, eb2, sw1, sb1, sw2, sb2):
        import jax, jax.numpy as jnp
        import numpy as np
        NUM_EXPERTS = 4
        TOP_K = 2
        B, L, D = context_c.shape
        E, K = (NUM_EXPERTS, TOP_K)
        L_head = L_wrist = L // 3
        head = context_c[:, :L_head]
        wrist = context_c[:, L_head:L_head + L_wrist]
        proprio = context_c[:, L_head + L_wrist:]
        full_agg = context_c.mean(axis=1)
        hp_agg = jnp.concatenate([head, proprio], axis=1).mean(axis=1)
        wp_agg = jnp.concatenate([wrist, proprio], axis=1).mean(axis=1)
        gate_in = jnp.concatenate([full_agg, hp_agg, wp_agg], axis=-1)
        gate_logits = gate_in @ gate_w + gate_b
        mod = jax.nn.silu(time_cond) @ time_w + time_b
        scale, shift = jnp.split(mod, 2, axis=-1)
        gate_logits = gate_logits * (1.0 + scale) + shift
        gate_scores = jax.nn.softmax(gate_logits, axis=-1)
        topk_w, topk_i = jax.lax.top_k(gate_scores, K)
        topk_w = topk_w / (topk_w.sum(axis=-1, keepdims=True) + 1e-08)
        onehot = (topk_i[..., None] == jnp.arange(E)[None, None, :]).astype(context_c.dtype)
        w_be = jnp.sum(topk_w[..., None] * onehot, axis=1)
        mask = np.ones((E, L), dtype=np.float32)
        mask[1, L_head:L_head + L_wrist] = 0.0
        mask[2, :L_head] = 0.0
        mask = jnp.asarray(mask)
        out = jnp.zeros_like(context_c)
        for e in range(E):
            h = jax.nn.gelu(context_c @ ew1[e] + eb1[e], approximate=True)
            y = h @ ew2[e] + eb2[e]
            out = out + w_be[:, e][:, None, None] * mask[e][None, :, None] * y
        shared = jax.nn.gelu(context_c @ sw1 + sb1, approximate=True) @ sw2 + sb2
        return out + shared
    x = x + _L0_cond_ref(x, cond_1024, L0_cond_base_up, L0_cond_base_down, L0_cond_ln_gamma, L0_cond_ln_beta, L0_cond_W1, L0_cond_bias1, L0_cond_W2, L0_cond_bias2)
    x = x + _L1_cond_ref(x, cond_1024, L1_cond_gate_w, L1_cond_gate_b, L1_cond_time_w, L1_cond_time_b, L1_cond_ew1, L1_cond_eb1, L1_cond_ew2, L1_cond_eb2, L1_cond_sw1, L1_cond_sb1, L1_cond_sw2, L1_cond_sb2)
    return x

_drawn_inputs = setup_inputs


def setup_inputs(seed=0):
    import zlib

    import numpy as np

    out = dict(_drawn_inputs(seed))
    spreads = {'L0_cond_ln_gamma': (1.0, 0.2),
     'L0_cond_ln_beta': (0.0, 0.1),
     'L0_cond_bias1': (0.0, 0.1),
     'L0_cond_bias2': (0.0, 0.1),
     'L1_cond_gate_b': (0.0, 0.8),
     'L1_cond_time_b': (0.0, 0.8),
     'L1_cond_eb1': (0.0, 0.8),
     'L1_cond_eb2': (0.0, 0.8),
     'L1_cond_sb1': (0.0, 0.8),
     'L1_cond_sb2': (0.0, 0.8)}
    factors = {'L0_cond_base_up': 5.228, 'L0_cond_base_down': 4.968, 'L1_cond_time_w': 8.0}
    for name, (base, spread) in spreads.items():
        noise = np.random.default_rng([zlib.crc32(name.encode()), seed]).standard_normal(out[name].shape)
        drawn = base * np.exp(spread * noise) if base else spread * noise
        out[name] = jnp.asarray(drawn.astype(out[name].dtype))
    for name, factor in factors.items():
        out[name] = (out[name] * factor).astype(out[name].dtype)
    return out
```

```python
import concourse.bass as bass
from concourse import mybir
from contextlib import ExitStack

P = 128
B = 2
T = 1024
D = 256
KT = D // P
RANK = 8
E = 4
TOPK = 2
H = 1024
HT = H // P
PAIRS = HT // 2
THIRD = T // 3
THIRDS = 3
NB = THIRD + 1
BATCH_COLS = THIRDS * NB
COLS = B * BATCH_COLS
BLOCKS = B * THIRDS
W1C = KT * H
W2C = HT * D
BIASC = HT + KT
EXPERTC = BIASC + W1C + W2C
LN_EPS = 1e-5
BANK = 512

C_COND = 0
C_GAMMA = C_COND + KT * B
C_BETA = C_GAMMA + KT
C_BIAS1 = C_BETA + KT
C_TIMEW = C_BIAS1 + KT
C_GATEW = C_TIMEW + KT * 2 * E
C_W1 = C_GATEW + THIRDS * KT * E
SMALLC = C_W1 + KT * D

UP_BANKS = 4
DOWN_BANKS = 2
ACT_PAIRS = 2
SCALED = 1
MID_TILES = BLOCKS * KT
MID_PAIRS = BLOCKS


def build(nc, xT, small, gate_bias, w2, bias2, base, experts, out):
    fp32, f32r, i32 = mybir.dt.float32, mybir.dt.float32r, mybir.dt.int32
    ALU = mybir.AluOpType
    ACT = mybir.ActivationFunctionType
    AX = mybir.AxisListType
    ds = bass.ds

    ctx = ExitStack()
    with ctx:
        def sb(name, shape, dt=fp32, stack=ctx):
            return stack.enter_context(nc.sbuf_tensor(name, shape, dt))

        def pb(name, shape):
            return ctx.enter_context(nc.psum_tensor(name, shape, fp32))

        def sem(name):
            return ctx.enter_context(nc.semaphore(name))

        x = sb("x", [P, KT, COLS])
        x_hi = sb("x_hi", [P, KT, COLS], f32r)
        x_lo = sb("x_lo", [P, KT, COLS], f32r)
        landing = sb("landing", [P, EXPERTC])
        wa_hi = sb("wa_hi", [P, W1C + W2C], f32r)
        wa_lo = sb("wa_lo", [P, W1C + W2C], f32r)
        act_out = sb("act_out", [P, UP_BANKS, NB])
        bias_set = sb("bias_set", [P, 2, BIASC])
        par = sb("par", [P, SMALLC])
        gbias = sb("gbias", [P, 3 * E])
        ones = sb("ones", [P, P])
        diff = sb("diff", [P, KT, B])
        diff2 = sb("diff2", [P, KT, B])
        rstd = sb("rstd", [P, B])
        cnorm = sb("cnorm", [P, KT, B])
        silu_c = sb("silu_c", [P, KT, B])
        hcond = sb("hcond", [P, KT, B])
        mod_prod = sb("mod_prod", [P, B, KT, 2 * E])
        mod = sb("mod", [P, B, 2 * E])
        sums = sb("sums", [P, KT, B, THIRDS])
        aggs = sb("aggs", [P, THIRDS, KT, B])
        gate_prod = sb("gate_prod", [P, B, THIRDS * KT, E])
        z = sb("z", [P, B, E])
        probs = sb("probs", [P, B, E])
        eqt = sb("eqt", [P, B, E])
        red = sb("red", [P, B])
        rinv = sb("rinv", [P, B])
        top_v = sb("top_v", [P, B, TOPK])
        top_i = sb("top_i", [P, B, TOPK])
        top_int = sb("top_int", [P, B, TOPK], i32)
        is_e = sb("is_e", [P, B, TOPK])
        wmask = sb("wmask", [P, B * TOPK * THIRDS])
        wm4 = wmask[:, :].rearrange("p (b s t) -> p b s t", b=B, s=TOPK)
        idx_up = sb("idx_up", [P, E])
        idx_down = sb("idx_down", [P, E])

        mark = ExitStack()
        sub = ExitStack()
        w2_a = sb("w2_a", [P, RANK, KT, 2 * D], stack=sub)
        sub.close()
        mid_hi = sb("mid_hi", [P, KT, COLS], f32r, stack=mark)
        mid_lo = sb("mid_lo", [P, KT, COLS], f32r, stack=mark)
        w2_b = sb("w2_b", [P, RANK, KT, 2 * D], stack=mark)
        h_diag = sb("h_diag", [P, RANK * (P + 1)], stack=mark)
        lr_half = sb("lr_half", [64, 2 * D], stack=mark)
        lr = sb("lr", [64, 2, 2 * D], stack=mark)
        b2s = sb("b2s", [64, 2, 2 * D], stack=mark)
        base_w = sb("base_w", [P, 2, KT, D], stack=mark)
        eff = sb("eff", [P, B, KT, D], stack=mark)
        eff_hi = [sb(f"eff_hi{s}", [P, B, KT, D], f32r, stack=mark) for s in range(2)]
        eff_lo = [sb(f"eff_lo{s}", [P, B, KT, D], f32r, stack=mark) for s in range(2)]
        mark.close()
        wb_hi = sb("wb_hi", [P, W1C + W2C], f32r)
        wb_lo = sb("wb_lo", [P, W1C + W2C], f32r)
        h_hi = sb("h_hi", [P, 2, HT, NB], f32r)
        h_lo = sb("h_lo", [P, 2, HT, NB], f32r)
        scaled = sb("scaled", [P, KT, NB])

        sets = [(wa_hi, wa_lo), (wb_hi, wb_lo)]
        SET_A, SET_B = 0, 1

        up_ps = pb("up_ps", [P, UP_BANKS, BANK])
        down_ps = pb("down_ps", [P, DOWN_BANKS, KT, BANK])
        SUM_PS = up_ps[:, 0, 0:B]
        VAR_PS = up_ps[:, 0, B:2 * B]
        HC_PS = up_ps[:, 1, 0:KT * B]
        MOD_PS = up_ps[:, 2, 0:B * 2 * E]
        GATE_PS = down_ps[:, 0, 0, 0:B * E]
        LR_PS = down_ps[:, 0, 1, :]
        EFF_PS = [down_ps[:, 1, b, :] for b in range(B)]

        s_small = sem("small_loaded")
        s_w2 = [sem(f"w2_loaded{c}") for c in range(8)]
        s_aux = sem("aux_loaded")
        s_x = [sem(f"x_loaded{b}") for b in range(B)]
        s_w1land = sem("first_weights_landed")
        s_w2land = sem("second_weights_landed")
        s_out = sem("out_stored")
        s_const = sem("constants_set")
        s_diag0 = sem("diag_cleared")
        s_pe_small = sem("small_product_done")
        s_dve = sem("dve_step_done")
        s_act_small = sem("act_small_done")
        s_diag = sem("diag_ready")
        s_lr = sem("lowrank_product_done")
        s_lr_ready = sem("lowrank_ready")
        s_effps = sem("effective_product_done")
        s_eff = sem("effective_weights_ready")
        s_xsplit = sem("x_split")
        s_up = sem("up_product_done")
        s_gelu = sem("gelu_done")
        s_hi = sem("hi_written")
        s_split = sem("pair_split")
        s_down = sem("down_product_done")
        s_evac = sem("down_bank_free")
        s_x1hi = sem("layer0_hi_written")
        s_x1lo = sem("layer0_lo_written")
        s_gprod = sem("gate_products_ready")
        s_gate = sem("gate_logits_done")
        s_shift = sem("logits_shifted")
        s_exp = sem("gate_exp_done")
        s_route = sem("routing_ready")
        s_wset = sem("weight_set_ready")
        s_pool = sem("pool_step_done")
        s_acc = sem("expert_block_added")

        block = ctx.enter_context(nc.Block())

        def col(b, t):
            return b * BATCH_COLS + t * NB

        def slot_order():
            return [(s, t, s * THIRDS + t) for s in range(TOPK) for t in range(THIRDS)]

        @block.sync
        def _(sp):
            sp.dma_start(par[:, :], small).then_inc(s_small, 16)
            sp.dma_start(gbias[:, :], gate_bias.partition_broadcast(P)).then_inc(s_small, 16)

            def load_w2(dst, stage, c):
                n = RANK // 4
                sp.dma_start(dst[:, c * n:(c + 1) * n, :, :],
                             w2[stage, :, c * n:(c + 1) * n, :, :]).then_inc(s_w2[4 * stage + c], 16)
            for c in range(4):
                load_w2(w2_a, 0, c)
            sp.dma_start(b2s[:, :, :], bias2).then_inc(s_aux, 16)
            sp.dma_start(base_w[:, :, :, :], base).then_inc(s_aux, 16)
            for b in range(B):
                sp.dma_start(x[:, :, col(b, 0):col(b, THIRDS)],
                             xT[:, :, col(b, 0):col(b, THIRDS)]).then_inc(s_x[b], 16)
            for c in range(4):
                load_w2(w2_b, 1, c)

            def load_expert(n, src):
                if n:
                    sp.wait_ge(s_wset, 2 * n)
                sp.dma_start(landing[:, 0:BIASC + W1C], src[:, 0:BIASC + W1C]).then_inc(s_w1land, 16)
                sp.dma_start(landing[:, BIASC + W1C:EXPERTC],
                             src[:, BIASC + W1C:EXPERTC]).then_inc(s_w2land, 16)

            load_expert(0, experts[E, :, :])
            sp.wait_ge(s_route, 1)
            for b in range(B):
                for s in range(TOPK):
                    e = sp.value_load(top_int[0:1, b, s:s + 1], min_val=0, max_val=E - 1)
                    load_expert(1 + b * TOPK + s,
                                experts[ds(e, 1), :, :].rearrange("e p n -> (e p) n"))
            for b in range(B):
                for t in range(THIRDS):
                    sp.wait_ge(s_acc, b * BLOCKS + (TOPK - 1) * THIRDS + t + 1 + SCALED)
                    c = col(b, t)
                    sp.dma_start(out[:, :, c:c + NB], x[:, :, c:c + NB]).then_inc(s_out, 16)
            sp.wait_ge(s_out, 16 * BLOCKS)

        @block.gpsimd
        def _(pool):
            nc.gpsimd.memset(ones[:, :], 1.0)
            for e in range(E):
                nc.gpsimd.memset(idx_up[:, e:e + 1], float(e))
                nc.gpsimd.memset(idx_down[:, e:e + 1], float(E - e))
            nc.gpsimd.memset(h_diag[:, :], 0.0).then_inc(s_const, 1)

            steps = [0]

            def split(n, weight_set, hi_done):
                hi, lo = sets[weight_set]
                pool.wait_ge(s_w1land, 16 * (n + 1))
                nc.gpsimd.tensor_scalar(bias_set[:, weight_set, :], landing[:, 0:BIASC], 1.0, 0.0,
                                        ALU.mult, ALU.add)
                for half, (a, w) in enumerate(((0, W1C), (W1C, W2C))):
                    if half:
                        pool.wait_ge(s_w2land, 16 * (n + 1))
                    src = landing[:, BIASC + a:BIASC + a + w]
                    nc.gpsimd.tensor_scalar(hi[:, a:a + w], src, 1.0, 0.0, ALU.mult,
                                            ALU.add).then_inc(s_pool, 1)
                    pool.wait_ge(s_pool, hi_done + half + 1)
                    nc.gpsimd.tensor_tensor(lo[:, a:a + w], src, hi[:, a:a + w].bitcast(fp32),
                                            ALU.subtract).then_inc(s_wset, 1)

            split(0, SET_A, 0)
            for b in range(B):
                pool.wait_ge(s_evac, DOWN_BANKS + BLOCKS + b * (BLOCKS + THIRDS))
                split(1 + b * TOPK, SET_B, 2 + b * 2 * TOPK)
                pool.wait_ge(s_evac, DOWN_BANKS + 2 * BLOCKS + b * BLOCKS)
                split(2 + b * TOPK, SET_A, 4 + b * 2 * TOPK)

        @block.scalar
        def _(act):
            act.sem_inc(s_gelu, UP_BANKS)
            act.wait_ge(s_small, 32)
            cond = par[:, C_COND:C_COND + KT * B].rearrange("p (k b) -> p k b", k=KT)
            nc.scalar.activation(silu_c[:, :, :], cond, ACT.Silu).then_inc(s_act_small, 1)
            act.wait_ge(s_dve, 4)
            nc.scalar.activation(rstd[:, :], rstd[:, :], ACT.Sqrt).then_inc(s_act_small, 1)
            act.wait_ge(s_pe_small, 3)
            for k in range(KT):
                last = nc.scalar.activation(hcond[:, k, :], HC_PS[:, k * B:(k + 1) * B], ACT.Gelu,
                                            bias=par[:, C_BIAS1 + k:C_BIAS1 + k + 1])
            last.then_inc(s_act_small, 1)

            def gelu_tile(k, ht, pair, func, **bias):
                if ht % 2 == 0:
                    act.wait_ge(s_split, pair + 1)
                act.wait_ge(s_up, k + 1)
                nc.scalar.activation(act_out[:, ht % UP_BANKS, :], up_ps[:, ht % UP_BANKS, 0:NB],
                                     func, **bias).then_inc(s_gelu, 1)

            with act.Fori(0, THIRDS) as i:
                for b in range(B):
                    for lt in range(KT):
                        gelu_tile(i * (B * KT) + (b * KT + lt), b * KT + lt, i * B + b, ACT.Gelu)

            with act.Fori(0, THIRDS) as i:
                for b in range(B):
                    act.wait_ge(s_evac, i * B + (b + 1 + DOWN_BANKS))
                    for k in range(KT):
                        c = i * NB + col(b, 0)
                        last = nc.scalar.activation(
                            x_hi[:, k, ds(c, NB)], x[:, k, ds(c, NB)], ACT.Identity,
                            accum_out=sums[:, k, b, ds(i, 1)])
                    last.then_inc(s_x1hi, 1)

            def expert_gelu(n, weight_set):
                for ht in range(HT):
                    gelu_tile(n * HT + (MID_TILES + ht), ht, n * PAIRS + (MID_PAIRS + ht // 2),
                              ACT.Gelu_apprx_tanh, bias=bias_set[:, weight_set, ht:ht + 1])

            for b in range(B):
                expert_gelu(b, SET_A)
                if b == 0:
                    act.wait_ge(s_shift, 1)
                    nc.scalar.activation(probs[:, :, :], z[:, :, :], ACT.Exp).then_inc(s_exp, 1)
            with act.Fori(1, THIRDS) as i:
                for b in range(B):
                    expert_gelu(i * B + b, SET_A)
            with act.Fori(0, B) as b:
                for s, t, m in slot_order():
                    expert_gelu(b * BLOCKS + (BLOCKS + m), SET_B if s == 0 else SET_A)

        @block.vector
        def _(dve):
            dve.sem_inc(s_split, ACT_PAIRS)
            dve.sem_inc(s_evac, DOWN_BANKS)
            dve.sem_inc(s_acc, SCALED)
            done = [0]

            def step(ins):
                done[0] += 1
                ins.then_inc(s_dve, 1)
                dve.wait_ge(s_dve, done[0])

            v = nc.vector
            cond = par[:, C_COND:C_COND + KT * B].rearrange("p (k b) -> p k b", k=KT)

            def over_k(a):
                return a.unsqueeze(1).to_broadcast([P, KT, B])

            dve.wait_ge(s_pe_small, 1)
            step(v.tensor_scalar(red[:, :], SUM_PS, 1.0 / D, None, ALU.mult))
            step(v.tensor_tensor(diff[:, :, :], cond, over_k(red[:, :]), ALU.subtract))
            step(v.tensor_tensor(diff2[:, :, :], diff[:, :, :], diff[:, :, :], ALU.mult))
            dve.wait_ge(s_pe_small, 2)
            step(v.tensor_scalar(rstd[:, :], VAR_PS, 1.0 / D, LN_EPS, ALU.mult, ALU.add))
            dve.wait_ge(s_act_small, 2)
            step(v.reciprocal(rinv[:, :], rstd[:, :]))
            step(v.tensor_tensor(cnorm[:, :, :], diff[:, :, :], over_k(rinv[:, :]), ALU.mult))
            for k in range(KT):
                last = v.tensor_scalar(cnorm[:, k, :], cnorm[:, k, :],
                                       par[:, C_GAMMA + k:C_GAMMA + k + 1],
                                       par[:, C_BETA + k:C_BETA + k + 1], ALU.mult, ALU.add)
            step(last)
            timew = par[:, C_TIMEW:C_TIMEW + KT * 2 * E].rearrange("p (k n) -> p k n", k=KT)
            step(v.tensor_tensor(
                mod_prod[:, :, :, :],
                timew.unsqueeze(1).to_broadcast([P, B, KT, 2 * E]),
                silu_c[:, :, :].rearrange("p k b -> p b k").unsqueeze(3).to_broadcast([P, B, KT, 2 * E]),
                ALU.mult))
            dve.wait_ge(s_act_small, 3)
            dve.wait_ge(s_const, 1)
            diag = h_diag[:, :].rearrange("p (r q) -> p r q", r=RANK)[:, :, 0:P:32]
            v.tensor_copy(diag, hcond[:, :, :].rearrange("p k b -> p (k b)").unsqueeze(1)
                          .to_broadcast([P, RANK, KT * B])).then_inc(s_diag, 1)
            dve.wait_ge(s_pe_small, 4)
            step(v.tensor_tensor(mod[:, :, :], MOD_PS.rearrange("p (b n) -> p b n", b=B),
                                 gbias[:, E:3 * E].unsqueeze(1).to_broadcast([P, B, 2 * E]), ALU.add))
            step(v.tensor_scalar(mod[:, :, 0:E], mod[:, :, 0:E], 1.0, None, ALU.add))

            def effective(stage):
                dve.wait_ge(s_lr, stage + 1)
                step(v.tensor_tensor(lr_half[:, :], LR_PS[64:128, :], b2s[:, stage, :], ALU.add))
                v.tensor_tensor(lr[:, stage, :], LR_PS[0:64, :], lr_half[:, :],
                                ALU.add).then_inc(s_lr_ready, 1)
                dve.wait_ge(s_effps, stage + 1)
                for b in range(B):
                    step(v.tensor_tensor(eff[:, b, :, :],
                                         EFF_PS[b].rearrange("p (k n) -> p k n", k=KT),
                                         base_w[:, stage, :, :], ALU.add))
                    step(v.tensor_copy(eff_hi[stage][:, b, :, :], eff[:, b, :, :]))
                    v.tensor_tensor(eff_lo[stage][:, b, :, :], eff[:, b, :, :],
                                    eff_hi[stage][:, b, :, :].bitcast(fp32),
                                    ALU.subtract).then_inc(s_eff, 1)

            dve.wait_ge(s_aux, 32)
            effective(0)
            for b in range(B):
                dve.wait_ge(s_x[b], 16)
                c0, c1 = col(b, 0), col(b, THIRDS)
                step(v.tensor_copy(x_hi[:, :, c0:c1], x[:, :, c0:c1]))
                v.tensor_tensor(x_lo[:, :, c0:c1], x[:, :, c0:c1], x_hi[:, :, c0:c1].bitcast(fp32),
                                ALU.subtract).then_inc(s_xsplit, 1)

            def split_pair(pair, place, hi, lo):
                src = act_out[:, 2 * place:2 * place + 2, :]
                dve.wait_ge(s_gelu, pair * 2 + (2 + UP_BANKS))
                v.tensor_copy(hi, src).then_inc(s_hi, 1)
                dve.wait_ge(s_hi, pair + 1)
                v.tensor_tensor(lo, src, hi.bitcast(fp32), ALU.subtract).then_inc(s_split, 1)

            with dve.Fori(0, THIRDS) as i:
                for b in range(B):
                    c = i * NB + col(b, 0)
                    split_pair(i * B + b, b, mid_hi[:, :, ds(c, NB)], mid_lo[:, :, ds(c, NB)])

            effective(1)

            with dve.Fori(0, THIRDS) as i:
                for b in range(B):
                    c = i * NB + col(b, 0)
                    dve.wait_ge(s_down, i * B + (b + 1))
                    v.scalar_tensor_tensor(x[:, :, ds(c, NB)], x[:, :, ds(c, NB)], 2.0,
                                           down_ps[:, b, :, 0:NB], ALU.mult,
                                           ALU.add).then_inc(s_evac, 1)
                for b in range(B):
                    c = i * NB + col(b, 0)
                    dve.wait_ge(s_x1hi, i * B + (b + 1))
                    v.tensor_tensor(x_lo[:, :, ds(c, NB)], x[:, :, ds(c, NB)],
                                    x_hi[:, :, ds(c, NB)].bitcast(fp32),
                                    ALU.subtract).then_inc(s_x1lo, 1)

            x5 = x[:, :, :].rearrange("p k (b t n) -> p k b t n", b=B, t=THIRDS)
            step(v.tensor_tensor(sums[:, :, :, 0:2], sums[:, :, :, 0:2], x5[:, :, :, 0:2, NB - 1],
                                 ALU.subtract))
            head, wrist, proprio = (sums[:, :, :, t] for t in range(THIRDS))
            v.tensor_tensor(aggs[:, 2, :, :], wrist, proprio, ALU.add)
            step(v.tensor_tensor(aggs[:, 1, :, :], head, proprio, ALU.add))
            step(v.tensor_tensor(aggs[:, 0, :, :], aggs[:, 1, :, :], wrist, ALU.add))
            v.tensor_scalar(aggs[:, 0, :, :], aggs[:, 0, :, :], 1.0 / T, None, ALU.mult)
            step(v.tensor_scalar(aggs[:, 1:3, :, :], aggs[:, 1:3, :, :], 1.0 / (T - THIRD), None,
                                 ALU.mult))
            gatew = par[:, C_GATEW:C_GATEW + THIRDS * KT * E].rearrange("p (c e) -> p c e", e=E)
            full = [P, B, THIRDS * KT, E]
            v.tensor_tensor(gate_prod[:, :, :, :], gatew.unsqueeze(1).to_broadcast(full),
                            aggs[:, :, :, :].rearrange("p g k b -> p b (g k)").unsqueeze(3)
                            .to_broadcast(full), ALU.mult).then_inc(s_gprod, 1)

            def over_e(a):
                return a.unsqueeze(2).to_broadcast([P, B, E])

            def over_b(a):
                return a.unsqueeze(1).to_broadcast([P, B, E])

            def route_logits():
                dve.wait_ge(s_gate, 1)
                step(v.tensor_tensor(z[:, :, :], GATE_PS.rearrange("p (b e) -> p b e", b=B),
                                     over_b(gbias[:, 0:E]), ALU.add))
                step(v.tensor_tensor(z[:, :, :], z[:, :, :], mod[:, :, 0:E], ALU.mult))
                step(v.tensor_tensor(z[:, :, :], z[:, :, :], mod[:, :, E:2 * E], ALU.add))
                step(v.tensor_reduce(red[:, :], z[:, :, :], AX.X, ALU.max))
                v.tensor_tensor(z[:, :, :], z[:, :, :], over_e(red[:, :]),
                                ALU.subtract).then_inc(s_shift, 1)

            def route_topk():
                dve.wait_ge(s_exp, 1)
                step(v.tensor_reduce(red[:, :], probs[:, :, :], AX.X, ALU.add))
                step(v.reciprocal(rinv[:, :], red[:, :]))
                step(v.tensor_tensor(probs[:, :, :], probs[:, :, :], over_e(rinv[:, :]), ALU.mult))
                for s in range(TOPK):
                    step(v.tensor_reduce(top_v[:, :, s], probs[:, :, :], AX.X, ALU.max))
                    step(v.tensor_tensor(eqt[:, :, :], probs[:, :, :], over_e(top_v[:, :, s]),
                                         ALU.is_equal))
                    step(v.tensor_tensor(eqt[:, :, :], eqt[:, :, :], over_b(idx_down[:, :]), ALU.mult))
                    step(v.tensor_reduce(red[:, :], eqt[:, :, :], AX.X, ALU.max))
                    step(v.tensor_scalar(top_i[:, :, s], red[:, :], -1.0, float(E), ALU.mult, ALU.add))
                    if s == 0:
                        step(v.tensor_tensor(eqt[:, :, :], over_b(idx_up[:, :]),
                                             over_e(top_i[:, :, s]), ALU.is_equal))
                        step(v.scalar_tensor_tensor(probs[:, :, :], eqt[:, :, :], -2.0,
                                                    probs[:, :, :], ALU.mult, ALU.add))
                v.tensor_copy(top_int[:, :, :], top_i[:, :, :]).then_inc(s_route, 1)
                step(v.tensor_tensor(red[:, :], top_v[:, :, 0], top_v[:, :, 1], ALU.add))
                step(v.tensor_scalar(red[:, :], red[:, :], 1e-8, None, ALU.add))
                step(v.reciprocal(rinv[:, :], red[:, :]))
                weight = wm4[:, :, :, 2]
                step(v.tensor_tensor(weight, top_v[:, :, :],
                                     rinv[:, :].unsqueeze(2).to_broadcast([P, B, TOPK]), ALU.mult))
                for t, e in ((0, 2), (1, 1)):
                    step(v.tensor_scalar(is_e[:, :, :], top_i[:, :, :], float(e), None, ALU.is_equal))
                    step(v.tensor_tensor(is_e[:, :, :], is_e[:, :, :], weight, ALU.mult))
                    step(v.tensor_tensor(wm4[:, :, :, t], weight, is_e[:, :, :], ALU.subtract))

            def expert_splits(n, parity):
                dve.wait_ge(s_down, n + (BLOCKS - 1))
                for q in range(PAIRS):
                    split_pair(n * PAIRS + (MID_PAIRS + q), q % 2,
                               h_hi[:, parity, 2 * q:2 * q + 2, :], h_lo[:, parity, 2 * q:2 * q + 2, :])

            def add_shared(n, b, c):
                dve.wait_ge(s_down, n + (BLOCKS + 1))
                for k in range(KT):
                    last = v.scalar_tensor_tensor(
                        x[:, k, ds(c, NB)], down_ps[:, b, k, 0:NB],
                        bias_set[:, SET_A, HT + k:HT + k + 1], x[:, k, ds(c, NB)], ALU.add, ALU.add)
                last.then_inc(s_evac, 1)

            def add_expert(n, done_before, parity, weight_set, w_at, c):
                dve.wait_ge(s_acc, done_before + SCALED)
                dve.wait_ge(s_down, n + (BLOCKS + 1))
                for k in range(KT):
                    last = v.tensor_scalar(scaled[:, k, :], down_ps[:, parity, k, 0:NB],
                                           bias_set[:, weight_set, HT + k:HT + k + 1],
                                           wmask[:, ds(w_at, 1)], ALU.add, ALU.mult)
                last.then_inc(s_evac, 1)
                dve.wait_ge(s_evac, n + (BLOCKS + 1 + DOWN_BANKS))
                v.tensor_tensor(x[:, :, ds(c, NB)], x[:, :, ds(c, NB)], scaled[:, :, :],
                                ALU.add).then_inc(s_acc, 1)

            expert_splits(0, 0)
            route_logits()
            expert_splits(1, 1)
            route_topk()
            for b in range(B):
                add_shared(b, b, col(b, 0))
            with dve.Fori(1, THIRDS) as i:
                for b in range(B):
                    expert_splits(i * B + b, b)
                for b in range(B):
                    add_shared(i * B + b, b, i * NB + col(b, 0))
            with dve.Fori(0, B) as b:
                order = slot_order()
                for s, t, m in order + [(None, None, BLOCKS)]:
                    if m < BLOCKS:
                        expert_splits(b * BLOCKS + (BLOCKS + m), m % 2)
                    if m:
                        s, t, m = order[m - 1]
                        add_expert(b * BLOCKS + (BLOCKS + m), b * BLOCKS + m, m % 2, SET_B if s == 0 else SET_A,
                                   b * (TOPK * THIRDS) + (s * THIRDS + t),
                                   b * BATCH_COLS + t * NB)

        @block.tensor
        def _(pe):
            mm = nc.tensor.matmul

            def product(dst, w_hi, w_lo, v_hi, v_lo, start, stop):
                mm(dst, w_lo, v_hi, start=start, stop=False)
                mm(dst, w_hi, v_hi, start=False, stop=False)
                return mm(dst, w_hi, v_lo, start=False, stop=stop)

            pe.wait_ge(s_small, 32)
            pe.wait_ge(s_const, 1)
            cond = par[:, C_COND:C_COND + KT * B].rearrange("p (k b) -> p k b", k=KT)
            for k in range(KT):
                last = mm(SUM_PS, ones[:, :], cond[:, k, :], start=k == 0, stop=k == KT - 1)
            last.then_inc(s_pe_small, 1)
            pe.wait_ge(s_dve, 3)
            for k in range(KT):
                last = mm(VAR_PS, ones[:, :], diff2[:, k, :], start=k == 0, stop=k == KT - 1)
            last.then_inc(s_pe_small, 1)
            pe.wait_ge(s_dve, 7)
            for n in range(KT):
                for k in range(KT):
                    at = C_W1 + k * D + n * P
                    last = mm(HC_PS[:, n * B:(n + 1) * B], par[:, at:at + P], cnorm[:, k, :],
                              start=k == 0, stop=k == KT - 1)
            last.then_inc(s_pe_small, 1)
            pe.wait_ge(s_dve, 8)
            for k in range(KT):
                last = mm(MOD_PS, ones[:, :], mod_prod[:, :, k, :], start=k == 0, stop=k == KT - 1)
            last.then_inc(s_pe_small, 1)

            def generate(stage, w2_sb):
                for r in range(RANK):
                    if r % 2 == 0:
                        pe.wait_ge(s_w2[4 * stage + r // 2], 16)
                    for g in range(KT * B):
                        at = r * P + g * 32
                        last = mm(LR_PS[32 * g:32 * g + 32, :], h_diag[:, at:at + 32],
                                  w2_sb[:, r, g // B, :], start=r == 0, stop=r == RANK - 1)
                last.then_inc(s_lr, 1)
                pe.wait_ge(s_lr_ready, stage + 1)
                for k in range(KT):
                    for b in range(B):
                        rows = lr[32 * b:32 * b + 32, stage, :]
                        last = mm(EFF_PS[b][:, k * D:(k + 1) * D], rows[:, k * P:(k + 1) * P],
                                  rows[:, D:2 * D], start=True, stop=True)
                last.then_inc(s_effps, 1)

            pe.wait_ge(s_diag, 1)
            generate(0, w2_a)

            pe.wait_ge(s_eff, 2)
            pe.wait_ge(s_xsplit, 2)
            with pe.Fori(0, THIRDS) as i:
                for b in range(B):
                    c = i * NB + col(b, 0)
                    for lt in range(KT):
                        pe.wait_ge(s_gelu, i * (B * KT) + (b * KT + lt + 1))
                        for k in range(KT):
                            n = slice(lt * P, (lt + 1) * P)
                            last = product(up_ps[:, b * KT + lt, 0:NB], eff_hi[0][:, b, k, n],
                                           eff_lo[0][:, b, k, n], x_hi[:, k, ds(c, NB)],
                                           x_lo[:, k, ds(c, NB)], k == 0, k == KT - 1)
                        last.then_inc(s_up, 1)

            generate(1, w2_b)

            pe.wait_ge(s_eff, 4)
            with pe.Fori(0, THIRDS) as i:
                for b in range(B):
                    c = i * NB + col(b, 0)
                    pe.wait_ge(s_split, i * B + (b + 1 + ACT_PAIRS))
                    pe.wait_ge(s_evac, i * B + (b + 1))
                    for dt in range(KT):
                        for k in range(KT):
                            n = slice(dt * P, (dt + 1) * P)
                            last = product(down_ps[:, b, dt, 0:NB], eff_hi[1][:, b, k, n],
                                           eff_lo[1][:, b, k, n], mid_hi[:, k, ds(c, NB)],
                                           mid_lo[:, k, ds(c, NB)], k == 0, k == KT - 1)
                    last.then_inc(s_down, 1)

            def expert_up(n, weight_set, c):
                hi, lo = sets[weight_set]
                for ht in range(HT):
                    pe.wait_ge(s_gelu, n * HT + (MID_TILES + ht + 1))
                    for k in range(KT):
                        at = k * H + ht * P
                        last = product(up_ps[:, ht % UP_BANKS, 0:NB], hi[:, at:at + P],
                                       lo[:, at:at + P], x_hi[:, k, ds(c, NB)],
                                       x_lo[:, k, ds(c, NB)], k == 0, k == KT - 1)
                    last.then_inc(s_up, 1)

            def expert_down(n, parity, weight_set):
                hi, lo = sets[weight_set]
                pe.wait_ge(s_evac, n + (BLOCKS + 1))
                for q in range(PAIRS):
                    pe.wait_ge(s_split, n * PAIRS + (MID_PAIRS + q + 1 + ACT_PAIRS))
                    for ht in (2 * q, 2 * q + 1):
                        for dt in range(KT):
                            at = W1C + ht * D + dt * P
                            last = product(down_ps[:, parity, dt, 0:NB], hi[:, at:at + P],
                                           lo[:, at:at + P], h_hi[:, parity, ht, :],
                                           h_lo[:, parity, ht, :], ht == 0, ht == HT - 1)
                last.then_inc(s_down, 1)

            pe.wait_ge(s_wset, 1)
            for b in range(B):
                pe.wait_ge(s_x1lo, b + 1)
                expert_up(b, SET_A, col(b, 0))
                if b == 0:
                    pe.wait_ge(s_gprod, 1)
                    pe.wait_ge(s_evac, BLOCKS + DOWN_BANKS)
                    for g in range(THIRDS * KT):
                        last = mm(GATE_PS, ones[:, :], gate_prod[:, :, g, :], start=g == 0,
                                  stop=g == THIRDS * KT - 1)
                    last.then_inc(s_gate, 1)
            pe.wait_ge(s_wset, 2)
            pe.wait_ge(s_shift, 1)
            for b in range(B):
                expert_down(b, b, SET_A)
            with pe.Fori(1, THIRDS) as i:
                for b in range(B):
                    pe.wait_ge(s_x1lo, i * B + (b + 1))
                    expert_up(i * B + b, SET_A, i * NB + col(b, 0))
                for b in range(B):
                    expert_down(i * B + b, b, SET_A)
            with pe.Fori(0, B) as b:
                order = slot_order()
                for s, t, m in order + [(None, None, BLOCKS)]:
                    if m < BLOCKS:
                        if t == 0:
                            pe.wait_ge(s_wset, b * (2 * TOPK) + (3 + 2 * s))
                        expert_up(b * BLOCKS + (BLOCKS + m), SET_B if s == 0 else SET_A,
                                  b * BATCH_COLS + t * NB)
                    if m:
                        s, t, m = order[m - 1]
                        if t == 0:
                            pe.wait_ge(s_wset, b * (2 * TOPK) + (4 + 2 * s))
                        expert_down(b * BLOCKS + (BLOCKS + m), m % 2, SET_B if s == 0 else SET_A)


def kernel(**inputs):
    import numpy as np
    import concourse.bacc as bacc
    from concourse.bass_utils import run_bass_kernel_spmd as run

    a = {k: np.asarray(v) for k, v in inputs.items()}

    def rows(w):
        return w.reshape(-1, P, w.shape[-1]).transpose(1, 0, 2).reshape(P, -1)

    def vec(v):
        return v.reshape(-1, P).T

    cuts = [slice(t * THIRD, t * THIRD + NB) for t in range(THIRDS)]
    xp = np.stack([a["x"][:, c] for c in cuts], axis=1)
    xT = xp.reshape(COLS, KT, P).transpose(2, 1, 0)
    small = np.concatenate([
        rows(a["cond_1024"].T), vec(a["L0_cond_ln_gamma"]), vec(a["L0_cond_ln_beta"]),
        vec(a["L0_cond_bias1"]), rows(a["L1_cond_time_w"]), rows(a["L1_cond_gate_w"]),
        rows(a["L0_cond_W1"])], axis=1)
    gate_bias = np.concatenate([a["L1_cond_gate_b"], a["L1_cond_time_b"]])
    parts = [2, 3, 1, 0]
    w2 = a["L0_cond_W2"].reshape(KT, P, 4, D, RANK)[:, :, parts]
    w2 = w2.reshape(KT, P, 2, 2, D, RANK).transpose(2, 1, 5, 0, 3, 4).reshape(2, P, RANK, KT, 2 * D)
    b2 = a["L0_cond_bias2"].reshape(4, D, RANK)[parts].reshape(2, 2 * D, RANK).transpose(2, 0, 1)
    bias2 = np.zeros((2, 32, 2, 2 * D), np.float32)
    bias2[:, 0:RANK] = b2
    bias2 = bias2.reshape(64, 2, 2 * D)
    base = np.stack([rows(a["L0_cond_base_down"]).reshape(P, KT, D),
                     rows(a["L0_cond_base_up"].T).reshape(P, KT, D)], axis=1)

    def expert(w1, b1, w2_, b2_):
        return np.concatenate([vec(b1), vec(b2_), rows(w1), rows(w2_)], axis=1)

    experts = np.stack(
        [expert(a["L1_cond_ew1"][e], a["L1_cond_eb1"][e], a["L1_cond_ew2"][e], a["L1_cond_eb2"][e])
         for e in range(E)]
        + [expert(a["L1_cond_sw1"], a["L1_cond_sb1"], a["L1_cond_sw2"], a["L1_cond_sb2"])])

    nc = bacc.Bacc("TRN2", target_bir_lowering=False, num_devices=1)
    arrays, aps = {}, []
    for name, value in (("xT", xT), ("small", small), ("gate_bias", gate_bias), ("w2", w2),
                        ("bias2", bias2), ("base", base), ("experts", experts)):
        arrays[name] = np.ascontiguousarray(value)
        aps.append(nc.dram_tensor(name, arrays[name].shape, mybir.dt.float32,
                                  kind="ExternalInput").ap())
    aps.append(nc.dram_tensor("yT", (P, KT, COLS), mybir.dt.float32, kind="ExternalOutput").ap())
    build(nc, *aps)
    y = run(nc, [arrays], core_ids=[0]).results[0]["yT"]
    y = y.transpose(2, 1, 0).reshape(B, THIRDS, NB, D)
    return np.concatenate([y[:, 0, 0:THIRD], y[:, 1, 0:THIRD], y[:, 2]], axis=1)
```

```python
import concourse.bass as bass
from concourse import mybir
from contextlib import ExitStack

P = 128
B = 2
T = 1024
D = 256
KT = D // P
RANK = 8
E = 4
TOPK = 2
HIDDEN_FROM = {0: 2, 1: 1}
H = 1024
HT = H // P
PAIRS = HT // 2
THIRD = T // 3
THIRDS = 3
NB = THIRD + 1
STEP = B * NB
COLS = THIRDS * STEP
BLOCKS = B * THIRDS
W1C = KT * H
W2C = HT * D
BIASC = HT + KT
EXPERTC = BIASC + W1C + W2C
LN_EPS = 1e-5
BANK = 512

C_COND = 0
C_GAMMA = C_COND + KT * B
C_BETA = C_GAMMA + KT
C_BIAS1 = C_BETA + KT
C_TIMEW = C_BIAS1 + KT
C_GATEW = C_TIMEW + KT * 2 * E
C_W1 = C_GATEW + THIRDS * KT * E
SMALLC = C_W1 + KT * D

UP_BANKS = 4
DOWN_BANKS = 2
ACT_PAIRS = 2
SCALED = 1
MID_TILES = BLOCKS * KT
MID_PAIRS = BLOCKS


def build(nc, xT, small, gate_bias, w2, bias2, base, experts, out):
    fp32, f32r, i32 = mybir.dt.float32, mybir.dt.float32r, mybir.dt.int32
    ALU = mybir.AluOpType
    ACT = mybir.ActivationFunctionType
    AX = mybir.AxisListType
    ds = bass.ds

    ctx = ExitStack()
    with ctx:
        def sb(name, shape, dt=fp32, stack=ctx):
            return stack.enter_context(nc.sbuf_tensor(name, shape, dt))

        def pb(name, shape):
            return ctx.enter_context(nc.psum_tensor(name, shape, fp32))

        def sem(name):
            return ctx.enter_context(nc.semaphore(name))

        x = sb("x", [P, KT, COLS])
        x_hi = sb("x_hi", [P, KT, COLS], f32r)
        x_lo = sb("x_lo", [P, KT, COLS], f32r)
        landing = sb("landing", [P, EXPERTC])
        wa_hi = sb("wa_hi", [P, W1C + W2C], f32r)
        wa_lo = sb("wa_lo", [P, W1C + W2C], f32r)
        act_out = sb("act_out", [P, UP_BANKS, NB])
        bias_set = sb("bias_set", [P, 2, BIASC])
        par = sb("par", [P, SMALLC])
        gbias = sb("gbias", [P, 3 * E])
        ones = sb("ones", [P, P])
        diff = sb("diff", [P, KT, B])
        diff2 = sb("diff2", [P, KT, B])
        rstd = sb("rstd", [P, B])
        cnorm = sb("cnorm", [P, KT, B])
        silu_c = sb("silu_c", [P, KT, B])
        hcond = sb("hcond", [P, KT, B])
        mod_prod = sb("mod_prod", [P, B, KT, 2 * E])
        mod = sb("mod", [P, B, 2 * E])
        sums = sb("sums", [P, THIRDS, KT, B])
        aggs = sb("aggs", [P, THIRDS, KT, B])
        gate_prod = sb("gate_prod", [P, B, THIRDS * KT, E])
        z = sb("z", [P, B, E])
        probs = sb("probs", [P, B, E])
        eqt = sb("eqt", [P, B, E])
        red = sb("red", [P, B])
        rinv = sb("rinv", [P, B])
        top_v = sb("top_v", [P, B, TOPK])
        top_i = sb("top_i", [P, B, TOPK])
        top_int = sb("top_int", [P, B, TOPK], i32)
        weights = sb("weights", [P, B * TOPK])
        idx_up = sb("idx_up", [P, E])
        idx_down = sb("idx_down", [P, E])

        mark = ExitStack()
        sub = ExitStack()
        w2_a = sb("w2_a", [P, RANK, KT, 2 * D], stack=sub)
        sub.close()
        mid_hi = sb("mid_hi", [P, KT, COLS], f32r, stack=mark)
        mid_lo = sb("mid_lo", [P, KT, COLS], f32r, stack=mark)
        w2_b = sb("w2_b", [P, RANK, KT, 2 * D], stack=mark)
        h_diag = sb("h_diag", [P, RANK * (KT * 32 + 1)], stack=mark)
        lr_half = sb("lr_half", [64, D], stack=mark)
        lr = sb("lr", [64, 2, D], stack=mark)
        lr_left = sb("lr_left", [64, 2, B, D], stack=mark)
        b2s = sb("b2s", [64, 2 * D + B], stack=mark)
        base_w = sb("base_w", [P, 2, KT, D], stack=mark)
        eff = sb("eff", [P, B, KT, D], stack=mark)
        eff_hi = [sb(f"eff_hi{s}", [P, B, KT, D], f32r, stack=mark) for s in range(2)]
        eff_lo = [sb(f"eff_lo{s}", [P, B, KT, D], f32r, stack=mark) for s in range(2)]
        mark.close()
        wb_hi = sb("wb_hi", [P, W1C + W2C], f32r)
        wb_lo = sb("wb_lo", [P, W1C + W2C], f32r)
        h_hi = sb("h_hi", [P, 2, HT, NB], f32r)
        h_lo = sb("h_lo", [P, 2, HT, NB], f32r)
        wbias = sb("wbias", [P, KT])

        sets = [(wa_hi, wa_lo), (wb_hi, wb_lo)]
        SET_A, SET_B = 0, 1

        up_ps = pb("up_ps", [P, UP_BANKS, BANK])
        down_ps = pb("down_ps", [P, DOWN_BANKS, KT, BANK])
        SUM_PS = up_ps[:, 0, 0:B]
        VAR_PS = up_ps[:, 0, B:2 * B]
        HC_PS = up_ps[:, 1, 0:KT * B]
        MOD_PS = up_ps[:, 2, 0:B * 2 * E]
        GATE_PS = down_ps[:, 0, 0, 0:B * E]
        LR_PS = down_ps[:, 0, 1, 0:D]
        EFF_PS = [down_ps[:, 1, b, :] for b in range(B)]

        s_small = sem("small_loaded")
        s_w2 = [sem(f"w2_loaded{c}") for c in range(8)]
        s_aux = sem("aux_loaded")
        s_x = [sem(f"x_loaded{t}") for t in range(THIRDS)]
        s_w1land = sem("first_weights_landed")
        s_w2land = sem("second_weights_landed")
        s_out = sem("out_stored")
        s_const = sem("constants_set")
        s_diag0 = sem("diag_cleared")
        s_pe_small = sem("small_product_done")
        s_dve = sem("dve_step_done")
        s_act_small = sem("act_small_done")
        s_diag = sem("diag_ready")
        s_lr = sem("lowrank_product_done")
        s_lr_ready = sem("lowrank_ready")
        s_effps = sem("effective_product_done")
        s_eff = sem("effective_weights_ready")
        s_xsplit = sem("x_thirds_split")
        s_up = sem("up_product_done")
        s_gelu = sem("gelu_done")
        s_hi = sem("hi_written")
        s_split = sem("pair_split")
        s_down = sem("down_product_done")
        s_evac = sem("down_bank_free")
        s_x1hi = sem("layer0_hi_written")
        s_x1lo = sem("layer0_lo_written")
        s_gprod = sem("gate_products_ready")
        s_gate = sem("gate_logits_done")
        s_shift = sem("logits_shifted")
        s_exp = sem("gate_exp_done")
        s_route = sem("routing_ready")
        s_wset = sem("weight_set_ready")
        s_pool = sem("pool_step_done")
        s_wbias = sem("weighted_bias_ready")
        s_acc = sem("bias_added")

        block = ctx.enter_context(nc.Block())

        def col(b, t):
            return t * STEP + b * NB

        def slot_order():
            return [(s, t, s * THIRDS + t) for s in range(TOPK) for t in range(THIRDS)]

        def chosen(eng, b):
            return [eng.value_load(top_int[0:1, ds(b, 1), s:s + 1], min_val=0, max_val=E - 1)
                    for s in range(TOPK)]

        def unless_hidden(eng, expert, t, work, skip):
            if t not in HIDDEN_FROM:
                work()
            else:
                with eng.If(expert != HIDDEN_FROM[t]):
                    work()
                with eng.Else():
                    skip()

        @block.sync
        def _(sp):
            sp.dma_start(par[:, :], small).then_inc(s_small, 16)
            sp.dma_start(gbias[:, :], gate_bias.partition_broadcast(P)).then_inc(s_small, 16)

            def load_w2(dst, stage, c):
                n = RANK // 4
                sp.dma_start(dst[:, c * n:(c + 1) * n, :, :],
                             w2[stage, :, c * n:(c + 1) * n, :, :]).then_inc(s_w2[4 * stage + c], 16)
            def load_x(t):
                n = slice(t * STEP, (t + 1) * STEP)
                sp.dma_start(x[:, :, n], xT[:, :, n]).then_inc(s_x[t], 16)

            load_x(0)
            for c in range(4):
                load_w2(w2_a, 0, c)
                if c == 0:
                    sp.dma_start(b2s[:, :], bias2).then_inc(s_aux, 16)
                    sp.dma_start(base_w[:, :, :, :], base).then_inc(s_aux, 16)
            for t in range(1, THIRDS):
                load_x(t)
            for c in range(4):
                load_w2(w2_b, 1, c)

            def load_expert(n, src):
                if n:
                    sp.wait_ge(s_wset, 2 * n)
                sp.dma_start(landing[:, 0:BIASC + W1C], src[:, 0:BIASC + W1C]).then_inc(s_w1land, 16)
                sp.dma_start(landing[:, BIASC + W1C:EXPERTC],
                             src[:, BIASC + W1C:EXPERTC]).then_inc(s_w2land, 16)

            load_expert(0, experts[E, :, :])
            sp.wait_ge(s_route, 1)
            for b in range(B):
                for s in range(TOPK):
                    e = sp.value_load(top_int[0:1, b, s:s + 1], min_val=0, max_val=E - 1)
                    load_expert(1 + b * TOPK + s,
                                experts[ds(e, 1), :, :].rearrange("e p n -> (e p) n"))
            for b in range(B):
                for t in range(THIRDS):
                    sp.wait_ge(s_evac, DOWN_BANKS + 2 * BLOCKS + b * BLOCKS + (TOPK - 1) * THIRDS + t + 1)
                    c = col(b, t)
                    sp.dma_start(out[:, :, c:c + NB], x[:, :, c:c + NB]).then_inc(s_out, 16)
            sp.wait_ge(s_out, 16 * BLOCKS)

        @block.gpsimd
        def _(pool):
            nc.gpsimd.memset(ones[:, :], 1.0)
            for e in range(E):
                nc.gpsimd.memset(idx_up[:, e:e + 1], float(e))
                nc.gpsimd.memset(idx_down[:, e:e + 1], float(E - e))
            nc.gpsimd.memset(h_diag[:, :], 0.0).then_inc(s_const, 1)

            hi_done = [0]

            def split(hi, lo, src, done):
                hi_done[0] += 1
                nc.gpsimd.tensor_scalar(hi, src, 1.0, 0.0, ALU.mult, ALU.add).then_inc(s_pool, 1)
                pool.wait_ge(s_pool, hi_done[0])
                nc.gpsimd.tensor_tensor(lo, src, hi.bitcast(fp32), ALU.subtract).then_inc(done, 1)

            pool.wait_ge(s_xsplit, 1)
            for t in range(1, THIRDS):
                pool.wait_ge(s_x[t], 16)
                n = slice(t * STEP, (t + 1) * STEP)
                split(x_hi[:, :, n], x_lo[:, :, n], x[:, :, n], s_xsplit)

            def split_expert(n, weight_set):
                hi, lo = sets[weight_set]
                pool.wait_ge(s_w1land, 16 * (n + 1))
                nc.gpsimd.tensor_scalar(bias_set[:, weight_set, :], landing[:, 0:BIASC], 1.0, 0.0,
                                        ALU.mult, ALU.add)
                split(hi[:, 0:W1C], lo[:, 0:W1C], landing[:, BIASC:BIASC + W1C], s_wset)
                pool.wait_ge(s_w2land, 16 * (n + 1))
                split(hi[:, W1C:W1C + W2C], lo[:, W1C:W1C + W2C], landing[:, BIASC + W1C:EXPERTC],
                      s_wset)

            split_expert(0, SET_A)
            for b in range(B):
                pool.wait_ge(s_evac, DOWN_BANKS + BLOCKS + b * (BLOCKS + THIRDS))
                split_expert(1 + b * TOPK, SET_B)
                pool.wait_ge(s_evac, DOWN_BANKS + 2 * BLOCKS + b * BLOCKS)
                split_expert(2 + b * TOPK, SET_A)

        @block.scalar
        def _(act):
            act.sem_inc(s_gelu, UP_BANKS)
            act.wait_ge(s_small, 32)
            cond = par[:, C_COND:C_COND + KT * B].rearrange("p (k b) -> p k b", k=KT)
            nc.scalar.activation(silu_c[:, :, :], cond, ACT.Silu).then_inc(s_act_small, 1)
            act.wait_ge(s_dve, 4)
            nc.scalar.activation(rstd[:, :], rstd[:, :], ACT.Sqrt).then_inc(s_act_small, 1)
            act.wait_ge(s_pe_small, 3)
            for k in range(KT):
                last = nc.scalar.activation(hcond[:, k, :], HC_PS[:, k * B:(k + 1) * B], ACT.Gelu,
                                            bias=par[:, C_BIAS1 + k:C_BIAS1 + k + 1])
            last.then_inc(s_act_small, 1)

            def gelu_tile(k, ht, pair, func, **bias):
                if ht % 2 == 0:
                    act.wait_ge(s_split, pair + 1)
                act.wait_ge(s_up, k + 1)
                nc.scalar.activation(act_out[:, ht % UP_BANKS, :], up_ps[:, ht % UP_BANKS, 0:NB],
                                     func, **bias).then_inc(s_gelu, 1)

            with act.Fori(0, THIRDS) as i:
                for b in range(B):
                    for lt in range(KT):
                        gelu_tile(i * (B * KT) + (b * KT + lt), b * KT + lt, i * B + b, ACT.Gelu)

            with act.Fori(0, THIRDS) as i:
                for b in range(B):
                    act.wait_ge(s_evac, i * B + (b + 1 + DOWN_BANKS))
                    for k in range(KT):
                        c = i * STEP + b * NB
                        last = nc.scalar.activation(
                            x_hi[:, k, ds(c, NB)], x[:, k, ds(c, NB)], ACT.Identity,
                            accum_out=sums[:, ds(i, 1), k, b])
                    last.then_inc(s_x1hi, 1)

            def expert_gelu(n, weight_set):
                for ht in range(HT):
                    gelu_tile(n * HT + (MID_TILES + ht), ht, n * PAIRS + (MID_PAIRS + ht // 2),
                              ACT.Gelu_apprx_tanh, bias=bias_set[:, weight_set, ht:ht + 1])

            for b in range(B):
                expert_gelu(b, SET_A)
                if b == 0:
                    act.wait_ge(s_shift, 1)
                    nc.scalar.activation(probs[:, :, :], z[:, :, :], ACT.Exp).then_inc(s_exp, 1)
            with act.Fori(1, THIRDS) as i:
                for b in range(B):
                    expert_gelu(i * B + b, SET_A)

            def skip_gelu():
                act.drain().then_inc(s_gelu, HT)

            act.wait_ge(s_route, 1)
            with act.Fori(0, B) as b:
                picked = chosen(act, b)
                for s, t, m in slot_order():
                    unless_hidden(
                        act, picked[s], t,
                        lambda: expert_gelu(b * BLOCKS + (BLOCKS + m), SET_B if s == 0 else SET_A),
                        skip_gelu)

        @block.vector
        def _(dve):
            dve.sem_inc(s_split, ACT_PAIRS)
            dve.sem_inc(s_evac, DOWN_BANKS)
            dve.sem_inc(s_acc, SCALED)
            done = [0]

            def step(ins):
                done[0] += 1
                ins.then_inc(s_dve, 1)
                dve.wait_ge(s_dve, done[0])

            v = nc.vector
            cond = par[:, C_COND:C_COND + KT * B].rearrange("p (k b) -> p k b", k=KT)

            def over_k(a):
                return a.unsqueeze(1).to_broadcast([P, KT, B])

            dve.wait_ge(s_pe_small, 1)
            step(v.tensor_scalar(red[:, :], SUM_PS, 1.0 / D, None, ALU.mult))
            step(v.tensor_tensor(diff[:, :, :], cond, over_k(red[:, :]), ALU.subtract))
            step(v.tensor_tensor(diff2[:, :, :], diff[:, :, :], diff[:, :, :], ALU.mult))
            dve.wait_ge(s_pe_small, 2)
            step(v.tensor_scalar(rstd[:, :], VAR_PS, 1.0 / D, LN_EPS, ALU.mult, ALU.add))
            dve.wait_ge(s_act_small, 2)
            step(v.reciprocal(rinv[:, :], rstd[:, :]))
            step(v.tensor_tensor(cnorm[:, :, :], diff[:, :, :], over_k(rinv[:, :]), ALU.mult))
            for k in range(KT):
                last = v.tensor_scalar(cnorm[:, k, :], cnorm[:, k, :],
                                       par[:, C_GAMMA + k:C_GAMMA + k + 1],
                                       par[:, C_BETA + k:C_BETA + k + 1], ALU.mult, ALU.add)
            step(last)
            timew = par[:, C_TIMEW:C_TIMEW + KT * 2 * E].rearrange("p (k n) -> p k n", k=KT)
            step(v.tensor_tensor(
                mod_prod[:, :, :, :],
                timew.unsqueeze(1).to_broadcast([P, B, KT, 2 * E]),
                silu_c[:, :, :].rearrange("p k b -> p b k").unsqueeze(3).to_broadcast([P, B, KT, 2 * E]),
                ALU.mult))
            dve.wait_ge(s_act_small, 3)
            dve.wait_ge(s_const, 1)
            diag = (h_diag[:, :].rearrange("p (r q) -> p r q", r=RANK)[:, :, 0:KT * 32]
                    .rearrange("p r (k m n) -> p r k m n", k=KT, n=RANK)[:, :, :, 0:B, 0])
            v.tensor_copy(diag, hcond[:, :, :].unsqueeze(1)
                          .to_broadcast([P, RANK, KT, B])).then_inc(s_diag, 1)
            dve.wait_ge(s_pe_small, 4)
            step(v.tensor_tensor(mod[:, :, :], MOD_PS.rearrange("p (b n) -> p b n", b=B),
                                 gbias[:, E:3 * E].unsqueeze(1).to_broadcast([P, B, 2 * E]), ALU.add))
            step(v.tensor_scalar(mod[:, :, 0:E], mod[:, :, 0:E], 1.0, None, ALU.add))

            dve.wait_ge(s_x[0], 16)
            step(v.tensor_copy(x_hi[:, :, 0:STEP], x[:, :, 0:STEP]))
            v.tensor_tensor(x_lo[:, :, 0:STEP], x[:, :, 0:STEP], x_hi[:, :, 0:STEP].bitcast(fp32),
                            ALU.subtract).then_inc(s_xsplit, 1)

            def factors(stage):
                dve.wait_ge(s_lr, stage + 1)
                step(v.tensor_tensor(lr_half[:, :], LR_PS[64:128, :],
                                     b2s[:, stage * D:(stage + 1) * D], ALU.add))
                step(v.tensor_tensor(lr[:, stage, :], LR_PS[0:64, :], lr_half[:, :], ALU.add))
                v.tensor_tensor(lr_left[32:64, stage, :, :],
                                lr[0:32, stage, :].unsqueeze(1).to_broadcast([32, B, D]),
                                b2s[0:32, 2 * D:2 * D + B].unsqueeze(2).to_broadcast([32, B, D]),
                                ALU.mult).then_inc(s_lr_ready, 1)

            def effective(stage):
                for b in range(B):
                    dve.wait_ge(s_effps, stage * B + b + 1)
                    step(v.tensor_tensor(eff[:, b, :, :],
                                         EFF_PS[b].rearrange("p (k n) -> p k n", k=KT),
                                         base_w[:, stage, :, :], ALU.add))
                    step(v.tensor_copy(eff_hi[stage][:, b, :, :], eff[:, b, :, :]))
                    v.tensor_tensor(eff_lo[stage][:, b, :, :], eff[:, b, :, :],
                                    eff_hi[stage][:, b, :, :].bitcast(fp32),
                                    ALU.subtract).then_inc(s_eff, 1)

            dve.wait_ge(s_aux, 32)
            factors(0)
            effective(0)

            def split_pair(pair, place, hi, lo):
                src = act_out[:, 2 * place:2 * place + 2, :]
                dve.wait_ge(s_gelu, pair * 2 + (2 + UP_BANKS))
                v.tensor_copy(hi, src).then_inc(s_hi, 1)
                dve.wait_ge(s_hi, pair + 1)
                v.tensor_tensor(lo, src, hi.bitcast(fp32), ALU.subtract).then_inc(s_split, 1)

            def mid_split(i, b):
                c = i * STEP + b * NB
                split_pair(i * B + b, b, mid_hi[:, :, ds(c, NB)], mid_lo[:, :, ds(c, NB)])

            with dve.Fori(0, THIRDS - 1) as i:
                for b in range(B):
                    mid_split(i, b)
            factors(1)
            mid_split(THIRDS - 1, 0)
            effective(1)
            mid_split(THIRDS - 1, 1)

            with dve.Fori(0, THIRDS) as i:
                for b in range(B):
                    c = i * STEP + b * NB
                    dve.wait_ge(s_down, i * B + (b + 1))
                    v.scalar_tensor_tensor(x[:, :, ds(c, NB)], x[:, :, ds(c, NB)], 2.0,
                                           down_ps[:, b, :, 0:NB], ALU.mult,
                                           ALU.add).then_inc(s_evac, 1)
                for b in range(B):
                    c = i * STEP + b * NB
                    dve.wait_ge(s_x1hi, i * B + (b + 1))
                    v.tensor_tensor(x_lo[:, :, ds(c, NB)], x[:, :, ds(c, NB)],
                                    x_hi[:, :, ds(c, NB)].bitcast(fp32),
                                    ALU.subtract).then_inc(s_x1lo, 1)

            x5 = x[:, :, :].rearrange("p k (t b n) -> p t k b n", b=B, t=THIRDS)
            step(v.tensor_tensor(sums[:, 0:2, :, :], sums[:, 0:2, :, :], x5[:, 0:2, :, :, NB - 1],
                                 ALU.subtract))
            head, wrist, proprio = (sums[:, t, :, :] for t in range(THIRDS))
            v.tensor_tensor(aggs[:, 2, :, :], wrist, proprio, ALU.add)
            step(v.tensor_tensor(aggs[:, 1, :, :], head, proprio, ALU.add))
            step(v.tensor_tensor(aggs[:, 0, :, :], aggs[:, 1, :, :], wrist, ALU.add))
            v.tensor_scalar(aggs[:, 0, :, :], aggs[:, 0, :, :], 1.0 / T, None, ALU.mult)
            step(v.tensor_scalar(aggs[:, 1:3, :, :], aggs[:, 1:3, :, :], 1.0 / (T - THIRD), None,
                                 ALU.mult))
            gatew = par[:, C_GATEW:C_GATEW + THIRDS * KT * E].rearrange("p (c e) -> p c e", e=E)
            full = [P, B, THIRDS * KT, E]
            v.tensor_tensor(gate_prod[:, :, :, :], gatew.unsqueeze(1).to_broadcast(full),
                            aggs[:, :, :, :].rearrange("p g k b -> p b (g k)").unsqueeze(3)
                            .to_broadcast(full), ALU.mult).then_inc(s_gprod, 1)

            def over_e(a):
                return a.unsqueeze(2).to_broadcast([P, B, E])

            def over_b(a):
                return a.unsqueeze(1).to_broadcast([P, B, E])

            def route_logits():
                dve.wait_ge(s_gate, 1)
                step(v.tensor_tensor(z[:, :, :], GATE_PS.rearrange("p (b e) -> p b e", b=B),
                                     over_b(gbias[:, 0:E]), ALU.add))
                step(v.tensor_tensor(z[:, :, :], z[:, :, :], mod[:, :, 0:E], ALU.mult))
                step(v.tensor_tensor(z[:, :, :], z[:, :, :], mod[:, :, E:2 * E], ALU.add))
                step(v.tensor_reduce(red[:, :], z[:, :, :], AX.X, ALU.max))
                v.tensor_tensor(z[:, :, :], z[:, :, :], over_e(red[:, :]),
                                ALU.subtract).then_inc(s_shift, 1)

            def route_topk():
                dve.wait_ge(s_exp, 1)
                step(v.tensor_reduce(red[:, :], probs[:, :, :], AX.X, ALU.add))
                step(v.reciprocal(rinv[:, :], red[:, :]))
                step(v.tensor_tensor(probs[:, :, :], probs[:, :, :], over_e(rinv[:, :]), ALU.mult))
                for s in range(TOPK):
                    step(v.tensor_reduce(top_v[:, :, s], probs[:, :, :], AX.X, ALU.max))
                    step(v.tensor_tensor(eqt[:, :, :], probs[:, :, :], over_e(top_v[:, :, s]),
                                         ALU.is_equal))
                    step(v.tensor_tensor(eqt[:, :, :], eqt[:, :, :], over_b(idx_down[:, :]), ALU.mult))
                    step(v.tensor_reduce(red[:, :], eqt[:, :, :], AX.X, ALU.max))
                    step(v.tensor_scalar(top_i[:, :, s], red[:, :], -1.0, float(E), ALU.mult, ALU.add))
                    if s == 0:
                        step(v.tensor_tensor(eqt[:, :, :], over_b(idx_up[:, :]),
                                             over_e(top_i[:, :, s]), ALU.is_equal))
                        step(v.scalar_tensor_tensor(probs[:, :, :], eqt[:, :, :], -2.0,
                                                    probs[:, :, :], ALU.mult, ALU.add))
                v.tensor_copy(top_int[:, :, :], top_i[:, :, :]).then_inc(s_route, 1)
                step(v.tensor_tensor(red[:, :], top_v[:, :, 0], top_v[:, :, 1], ALU.add))
                step(v.tensor_scalar(red[:, :], red[:, :], 1e-8, None, ALU.add))
                step(v.reciprocal(rinv[:, :], red[:, :]))
                step(v.tensor_tensor(weights[:, :].rearrange("p (b s) -> p b s", b=B),
                                     top_v[:, :, :],
                                     rinv[:, :].unsqueeze(2).to_broadcast([P, B, TOPK]), ALU.mult))

            def expert_splits(n, parity):
                dve.wait_ge(s_down, n + (BLOCKS - 1))
                for q in range(PAIRS):
                    split_pair(n * PAIRS + (MID_PAIRS + q), q % 2,
                               h_hi[:, parity, 2 * q:2 * q + 2, :], h_lo[:, parity, 2 * q:2 * q + 2, :])

            def add_shared(n, b, c):
                dve.wait_ge(s_down, n + (BLOCKS + 1))
                for k in range(KT):
                    last = v.scalar_tensor_tensor(
                        x[:, k, ds(c, NB)], down_ps[:, b, k, 0:NB],
                        bias_set[:, SET_A, HT + k:HT + k + 1], x[:, k, ds(c, NB)], ALU.add, ALU.add)
                last.then_inc(s_evac, 1)

            def add_expert(n, done_before, parity, weight_set, w_at, c):
                weight = weights[:, ds(w_at, 1)]
                dve.wait_ge(s_acc, done_before + SCALED)
                v.tensor_scalar(wbias[:, :], bias_set[:, weight_set, HT:HT + KT], weight, None,
                                ALU.mult).then_inc(s_wbias, 1)
                dve.wait_ge(s_wbias, done_before + 1)
                for k in range(KT):
                    last = v.tensor_scalar(x[:, k, ds(c, NB)], x[:, k, ds(c, NB)], wbias[:, k:k + 1],
                                           None, ALU.add)
                last.then_inc(s_acc, 1)
                dve.wait_ge(s_acc, done_before + 1 + SCALED)
                dve.wait_ge(s_down, n + (BLOCKS + 1))
                for k in range(KT):
                    last = v.scalar_tensor_tensor(x[:, k, ds(c, NB)], down_ps[:, parity, k, 0:NB],
                                                  weight, x[:, k, ds(c, NB)], ALU.mult, ALU.add)
                last.then_inc(s_evac, 1)

            expert_splits(0, 0)
            route_logits()
            expert_splits(1, 1)
            route_topk()
            for b in range(B):
                add_shared(b, b, col(b, 0))
            with dve.Fori(1, THIRDS) as i:
                for b in range(B):
                    expert_splits(i * B + b, b)
                for b in range(B):
                    add_shared(i * B + b, b, i * STEP + b * NB)

            def skip_splits():
                dve.drain().then_inc(s_hi, PAIRS)
                dve.drain().then_inc(s_split, PAIRS)

            def skip_add():
                dve.drain().then_inc(s_wbias, 1)
                dve.drain().then_inc(s_acc, 1)
                dve.drain().then_inc(s_evac, 1)

            dve.wait_ge(s_route, 1)
            with dve.Fori(0, B) as b:
                picked = chosen(dve, b)
                order = slot_order()
                for m in range(BLOCKS + 1):
                    if m < BLOCKS:
                        s, t, _ = order[m]
                        unless_hidden(
                            dve, picked[s], t,
                            lambda: expert_splits(b * BLOCKS + (BLOCKS + m), m % 2), skip_splits)
                    if m:
                        s, t, last = order[m - 1]
                        unless_hidden(
                            dve, picked[s], t,
                            lambda: add_expert(b * BLOCKS + (BLOCKS + last), b * BLOCKS + last,
                                               last % 2, SET_B if s == 0 else SET_A,
                                               b * TOPK + s, b * NB + t * STEP), skip_add)

        @block.tensor
        def _(pe):
            mm = nc.tensor.matmul

            def product(dst, w_hi, w_lo, v_hi, v_lo, start, stop):
                mm(dst, w_lo, v_hi, start=start, stop=False)
                mm(dst, w_hi, v_hi, start=False, stop=False)
                return mm(dst, w_hi, v_lo, start=False, stop=stop)

            pe.wait_ge(s_small, 32)
            pe.wait_ge(s_const, 1)
            cond = par[:, C_COND:C_COND + KT * B].rearrange("p (k b) -> p k b", k=KT)
            for k in range(KT):
                last = mm(SUM_PS, ones[:, :], cond[:, k, :], start=k == 0, stop=k == KT - 1)
            last.then_inc(s_pe_small, 1)
            pe.wait_ge(s_dve, 3)
            for k in range(KT):
                last = mm(VAR_PS, ones[:, :], diff2[:, k, :], start=k == 0, stop=k == KT - 1)
            last.then_inc(s_pe_small, 1)
            pe.wait_ge(s_dve, 7)
            for n in range(KT):
                for k in range(KT):
                    at = C_W1 + k * D + n * P
                    last = mm(HC_PS[:, n * B:(n + 1) * B], par[:, at:at + P], cnorm[:, k, :],
                              start=k == 0, stop=k == KT - 1)
            last.then_inc(s_pe_small, 1)
            pe.wait_ge(s_dve, 8)
            for k in range(KT):
                last = mm(MOD_PS, ones[:, :], mod_prod[:, :, k, :], start=k == 0, stop=k == KT - 1)
            last.then_inc(s_pe_small, 1)

            def low_rank(stage, w2_sb, chunks):
                for c in chunks:
                    pe.wait_ge(s_w2[4 * stage + c], 16)
                    for r in range(c * RANK // 4, (c + 1) * RANK // 4):
                        for k in range(KT):
                            for side in range(2):
                                at = r * KT * 32 + k * 32
                                row = 32 * (2 * k + side)
                                last = mm(LR_PS[row:row + 32, :], h_diag[:, at:at + 32],
                                          w2_sb[:, r, k, side * D:(side + 1) * D],
                                          start=r == 0, stop=r == RANK - 1)
                if c == 3:
                    last.then_inc(s_lr, 1)

            def fold(stage):
                pe.wait_ge(s_lr_ready, stage + 1)
                for b in range(B):
                    for k in range(KT):
                        last = mm(EFF_PS[b][:, k * D:(k + 1) * D],
                                  lr_left[32:64, stage, b, k * P:(k + 1) * P],
                                  lr[32:64, stage, :], start=True, stop=True)
                    last.then_inc(s_effps, 1)

            pe.wait_ge(s_diag, 1)
            low_rank(0, w2_a, range(4))
            fold(0)
            low_rank(1, w2_b, range(1))

            def mid_product(i, b):
                c = i * STEP + b * NB
                pe.wait_ge(s_eff, b + 1)
                pe.wait_ge(s_xsplit, i + 1)
                for lt in range(KT):
                    pe.wait_ge(s_gelu, i * (B * KT) + (b * KT + lt + 1))
                    for k in range(KT):
                        n = slice(lt * P, (lt + 1) * P)
                        last = product(up_ps[:, b * KT + lt, 0:NB], eff_hi[0][:, b, k, n],
                                       eff_lo[0][:, b, k, n], x_hi[:, k, ds(c, NB)],
                                       x_lo[:, k, ds(c, NB)], k == 0, k == KT - 1)
                    last.then_inc(s_up, 1)

            with pe.Fori(0, THIRDS - 1) as i:
                for b in range(B):
                    mid_product(i, b)
            low_rank(1, w2_b, range(1, 4))
            mid_product(THIRDS - 1, 0)
            fold(1)
            mid_product(THIRDS - 1, 1)

            with pe.Fori(0, THIRDS) as i:
                for b in range(B):
                    c = i * STEP + b * NB
                    pe.wait_ge(s_eff, B + b + 1)
                    pe.wait_ge(s_split, i * B + (b + 1 + ACT_PAIRS))
                    pe.wait_ge(s_evac, i * B + (b + 1))
                    for dt in range(KT):
                        for k in range(KT):
                            n = slice(dt * P, (dt + 1) * P)
                            last = product(down_ps[:, b, dt, 0:NB], eff_hi[1][:, b, k, n],
                                           eff_lo[1][:, b, k, n], mid_hi[:, k, ds(c, NB)],
                                           mid_lo[:, k, ds(c, NB)], k == 0, k == KT - 1)
                    last.then_inc(s_down, 1)

            def expert_up(n, weight_set, c):
                hi, lo = sets[weight_set]
                for ht in range(HT):
                    pe.wait_ge(s_gelu, n * HT + (MID_TILES + ht + 1))
                    for k in range(KT):
                        at = k * H + ht * P
                        last = product(up_ps[:, ht % UP_BANKS, 0:NB], hi[:, at:at + P],
                                       lo[:, at:at + P], x_hi[:, k, ds(c, NB)],
                                       x_lo[:, k, ds(c, NB)], k == 0, k == KT - 1)
                    last.then_inc(s_up, 1)

            def expert_down(n, parity, weight_set):
                hi, lo = sets[weight_set]
                pe.wait_ge(s_evac, n + (BLOCKS + 1))
                for q in range(PAIRS):
                    pe.wait_ge(s_split, n * PAIRS + (MID_PAIRS + q + 1 + ACT_PAIRS))
                    for ht in (2 * q, 2 * q + 1):
                        for dt in range(KT):
                            at = W1C + ht * D + dt * P
                            last = product(down_ps[:, parity, dt, 0:NB], hi[:, at:at + P],
                                           lo[:, at:at + P], h_hi[:, parity, ht, :],
                                           h_lo[:, parity, ht, :], ht == 0, ht == HT - 1)
                last.then_inc(s_down, 1)

            pe.wait_ge(s_wset, 1)
            for b in range(B):
                pe.wait_ge(s_x1lo, b + 1)
                expert_up(b, SET_A, col(b, 0))
                if b == 0:
                    pe.wait_ge(s_gprod, 1)
                    pe.wait_ge(s_evac, BLOCKS + DOWN_BANKS)
                    for g in range(THIRDS * KT):
                        last = mm(GATE_PS, ones[:, :], gate_prod[:, :, g, :], start=g == 0,
                                  stop=g == THIRDS * KT - 1)
                    last.then_inc(s_gate, 1)
            pe.wait_ge(s_wset, 2)
            pe.wait_ge(s_shift, 1)
            for b in range(B):
                expert_down(b, b, SET_A)
            with pe.Fori(1, THIRDS) as i:
                for b in range(B):
                    pe.wait_ge(s_x1lo, i * B + (b + 1))
                    expert_up(i * B + b, SET_A, i * STEP + b * NB)
                for b in range(B):
                    expert_down(i * B + b, b, SET_A)

            def skip_up():
                pe.drain().then_inc(s_up, HT)

            def skip_down():
                pe.drain().then_inc(s_down, 1)

            pe.wait_ge(s_route, 1)
            with pe.Fori(0, B) as b:
                picked = chosen(pe, b)
                order = slot_order()
                for m in range(BLOCKS + 1):
                    if m < BLOCKS:
                        s, t, _ = order[m]
                        if t == 0:
                            pe.wait_ge(s_wset, b * (2 * TOPK) + (3 + 2 * s))
                        unless_hidden(
                            pe, picked[s], t,
                            lambda: expert_up(b * BLOCKS + (BLOCKS + m), SET_B if s == 0 else SET_A,
                                              b * NB + t * STEP), skip_up)
                    if m:
                        s, t, last = order[m - 1]
                        if t == 0:
                            pe.wait_ge(s_wset, b * (2 * TOPK) + (4 + 2 * s))
                        unless_hidden(
                            pe, picked[s], t,
                            lambda: expert_down(b * BLOCKS + (BLOCKS + last), last % 2,
                                                SET_B if s == 0 else SET_A), skip_down)


def kernel(**inputs):
    import numpy as np
    import concourse.bacc as bacc
    from concourse.bass_utils import run_bass_kernel_spmd as run

    a = {k: np.asarray(v) for k, v in inputs.items()}

    def rows(w):
        return w.reshape(-1, P, w.shape[-1]).transpose(1, 0, 2).reshape(P, -1)

    def vec(v):
        return v.reshape(-1, P).T

    cuts = [slice(t * THIRD, t * THIRD + NB) for t in range(THIRDS)]
    xp = np.stack([a["x"][:, c] for c in cuts])
    xT = xp.reshape(COLS, KT, P).transpose(2, 1, 0)
    small = np.concatenate([
        rows(a["cond_1024"].T), vec(a["L0_cond_ln_gamma"]), vec(a["L0_cond_ln_beta"]),
        vec(a["L0_cond_bias1"]), rows(a["L1_cond_time_w"]), rows(a["L1_cond_gate_w"]),
        rows(a["L0_cond_W1"])], axis=1)
    gate_bias = np.concatenate([a["L1_cond_gate_b"], a["L1_cond_time_b"]])
    parts = [2, 3, 1, 0]
    w2 = a["L0_cond_W2"].reshape(KT, P, 4, D, RANK)[:, :, parts]
    w2 = w2.reshape(KT, P, 2, 2, D, RANK).transpose(2, 1, 5, 0, 3, 4).reshape(2, P, RANK, KT, 2 * D)
    b2 = a["L0_cond_bias2"].reshape(4, D, RANK)[parts].reshape(2, 2 * D, RANK).transpose(2, 0, 1)
    bias2 = np.zeros((2, 32, 2 * D + B), np.float32)
    for b in range(B):
        bias2[:, b * RANK:(b + 1) * RANK, 0:2 * D] = (
            b2.reshape(RANK, 2, 2, D).transpose(2, 0, 1, 3).reshape(2, RANK, 2 * D))
        bias2[:, b * RANK:(b + 1) * RANK, 2 * D + b] = 1
    bias2 = bias2.reshape(64, 2 * D + B)
    base = np.stack([rows(a["L0_cond_base_down"]).reshape(P, KT, D),
                     rows(a["L0_cond_base_up"].T).reshape(P, KT, D)], axis=1)

    def expert(w1, b1, w2_, b2_):
        return np.concatenate([vec(b1), vec(b2_), rows(w1), rows(w2_)], axis=1)

    experts = np.stack(
        [expert(a["L1_cond_ew1"][e], a["L1_cond_eb1"][e], a["L1_cond_ew2"][e], a["L1_cond_eb2"][e])
         for e in range(E)]
        + [expert(a["L1_cond_sw1"], a["L1_cond_sb1"], a["L1_cond_sw2"], a["L1_cond_sb2"])])

    nc = bacc.Bacc("TRN2", target_bir_lowering=False, num_devices=1)
    arrays, aps = {}, []
    for name, value in (("xT", xT), ("small", small), ("gate_bias", gate_bias), ("w2", w2),
                        ("bias2", bias2), ("base", base), ("experts", experts)):
        arrays[name] = np.ascontiguousarray(value)
        aps.append(nc.dram_tensor(name, arrays[name].shape, mybir.dt.float32,
                                  kind="ExternalInput").ap())
    aps.append(nc.dram_tensor("yT", (P, KT, COLS), mybir.dt.float32, kind="ExternalOutput").ap())
    build(nc, *aps)
    y = run(nc, [arrays], core_ids=[0]).results[0]["yT"]
    y = y.transpose(2, 1, 0).reshape(THIRDS, B, NB, D)
    return np.concatenate([y[0, :, 0:THIRD], y[1, :, 0:THIRD], y[2]], axis=1)
```

```python
import concourse.bass as bass
from concourse import mybir
from contextlib import ExitStack

P = 128
B = 2
T = 1024
D = 256
KT = D // P
RANK = 8
E = 4
TOPK = 2
HIDDEN_FROM = {0: 2, 1: 1}
H = 1024
HT = H // P
PAIRS = HT // 2
THIRD = T // 3
THIRDS = 3
NB = THIRD + 1
STEP = B * NB
COLS = THIRDS * STEP
BLOCKS = B * THIRDS
W1C = KT * H
W2C = HT * D
BIASC = HT + KT
EXPERTC = BIASC + W1C + W2C
LN_EPS = 1e-5
BANK = 512

C_COND = 0
C_GAMMA = C_COND + KT * B
C_BETA = C_GAMMA + KT
C_BIAS1 = C_BETA + KT
C_TIMEW = C_BIAS1 + KT
C_GATEW = C_TIMEW + KT * 2 * E
C_W1 = C_GATEW + THIRDS * KT * E
SMALLC = C_W1 + KT * D

RANK_CUTS = [0, 2, 4, 6, 7, 8]
CHUNKS = len(RANK_CUTS) - 1

UP_BANKS = 4
DOWN_BANKS = 2
ACT_PAIRS = 2
SCALED = 1
MID_TILES = BLOCKS * KT
MID_PAIRS = BLOCKS


def build(nc, xT, small, gate_bias, w2, bias2, base, experts, out):
    fp32, f32r, i32 = mybir.dt.float32, mybir.dt.float32r, mybir.dt.int32
    ALU = mybir.AluOpType
    ACT = mybir.ActivationFunctionType
    AX = mybir.AxisListType
    ds = bass.ds

    ctx = ExitStack()
    with ctx:
        def sb(name, shape, dt=fp32, stack=ctx):
            return stack.enter_context(nc.sbuf_tensor(name, shape, dt))

        def pb(name, shape):
            return ctx.enter_context(nc.psum_tensor(name, shape, fp32))

        def sem(name):
            return ctx.enter_context(nc.semaphore(name))

        x = sb("x", [P, KT, COLS])
        x_hi = sb("x_hi", [P, KT, COLS], f32r)
        x_lo = sb("x_lo", [P, KT, COLS], f32r)
        landing = sb("landing", [P, EXPERTC])
        wa_hi = sb("wa_hi", [P, W1C + W2C], f32r)
        wa_lo = sb("wa_lo", [P, W1C + W2C], f32r)
        act_out = sb("act_out", [P, UP_BANKS, NB])
        bias_set = sb("bias_set", [P, 2, BIASC])
        par = sb("par", [P, SMALLC])
        gbias = sb("gbias", [P, 3 * E])
        ones = sb("ones", [P, P])
        diff = sb("diff", [P, KT, B])
        diff2 = sb("diff2", [P, KT, B])
        rstd = sb("rstd", [P, B])
        cnorm = sb("cnorm", [P, KT, B])
        silu_c = sb("silu_c", [P, KT, B])
        hcond = sb("hcond", [P, KT, B])
        mod_prod = sb("mod_prod", [P, B, KT, 2 * E])
        mod = sb("mod", [P, B, 2 * E])
        sums = sb("sums", [P, THIRDS, KT, B])
        aggs = sb("aggs", [P, THIRDS, KT, B])
        gate_prod = sb("gate_prod", [P, B, THIRDS * KT, E])
        z = sb("z", [P, B, E])
        probs = sb("probs", [P, B, E])
        eqt = sb("eqt", [P, B, E])
        red = sb("red", [P, B])
        rinv = sb("rinv", [P, B])
        top_v = sb("top_v", [P, B, TOPK])
        top_i = sb("top_i", [P, B, TOPK])
        top_int = sb("top_int", [P, B, TOPK], i32)
        weights = sb("weights", [P, B * TOPK])
        idx_up = sb("idx_up", [P, E])
        idx_down = sb("idx_down", [P, E])

        mark = ExitStack()
        sub = ExitStack()
        w2_a = sb("w2_a", [P, RANK, KT, 2 * D], stack=sub)
        sub.close()
        mid_hi = sb("mid_hi", [P, KT, COLS], f32r, stack=mark)
        mid_lo = sb("mid_lo", [P, KT, COLS], f32r, stack=mark)
        w2_b = sb("w2_b", [P, RANK, KT, 2 * D], stack=mark)
        h_diag = sb("h_diag", [P, RANK * (KT * 32 + 1)], stack=mark)
        lr_half = sb("lr_half", [64, D], stack=mark)
        lr = sb("lr", [64, 2, D], stack=mark)
        lr_left = sb("lr_left", [64, 2, B, D], stack=mark)
        b2s = sb("b2s", [64, 2 * D + B], stack=mark)
        base_w = sb("base_w", [P, 2, KT, D], stack=mark)
        eff = sb("eff", [P, B, KT, D], stack=mark)
        eff_hi = [sb(f"eff_hi{s}", [P, B, KT, D], f32r, stack=mark) for s in range(2)]
        eff_lo = [sb(f"eff_lo{s}", [P, B, KT, D], f32r, stack=mark) for s in range(2)]
        mark.close()
        wb_hi = sb("wb_hi", [P, W1C + W2C], f32r)
        wb_lo = sb("wb_lo", [P, W1C + W2C], f32r)
        h_hi = sb("h_hi", [P, 2, HT, NB], f32r)
        h_lo = sb("h_lo", [P, 2, HT, NB], f32r)
        wbias = sb("wbias", [P, KT])

        sets = [(wa_hi, wa_lo), (wb_hi, wb_lo)]
        SET_A, SET_B = 0, 1

        up_ps = pb("up_ps", [P, UP_BANKS, BANK])
        down_ps = pb("down_ps", [P, DOWN_BANKS, KT, BANK])
        SUM_PS = up_ps[:, 0, 0:B]
        VAR_PS = up_ps[:, 0, B:2 * B]
        HC_PS = up_ps[:, 1, 0:KT * B]
        MOD_PS = up_ps[:, 2, 0:B * 2 * E]
        GATE_PS = down_ps[:, 0, 0, 0:B * E]
        LR_PS = down_ps[:, 0, 1, 0:D]
        EFF_PS = [down_ps[:, 1, b, :] for b in range(B)]

        s_small = sem("small_loaded")
        s_w2 = [sem(f"w2_loaded{c}") for c in range(2 * CHUNKS)]
        s_aux = sem("factor_bias_loaded")
        s_base = [sem(f"base_loaded{s}") for s in range(2)]
        s_x = [sem(f"x_loaded{t}") for t in range(THIRDS)]
        s_w1land = sem("first_weights_landed")
        s_w2land = sem("second_weights_landed")
        s_out = sem("out_stored")
        s_const = sem("constants_set")
        s_diag0 = sem("diag_cleared")
        s_pe_small = sem("small_product_done")
        s_dve = sem("dve_step_done")
        s_act_small = sem("act_small_done")
        s_diag = sem("diag_ready")
        s_lr = sem("lowrank_product_done")
        s_lr_ready = sem("lowrank_ready")
        s_effps = sem("effective_product_done")
        s_eff = sem("effective_weights_ready")
        s_xhi = sem("x_hi_written")
        s_xsplit = sem("x_split")
        s_up = sem("up_product_done")
        s_gelu = sem("gelu_done")
        s_hi = sem("hi_written")
        s_split = sem("pair_split")
        s_down = sem("down_product_done")
        s_evac = sem("down_bank_free")
        s_x1hi = sem("layer0_hi_written")
        s_x1lo = sem("layer0_lo_written")
        s_gprod = sem("gate_products_ready")
        s_gate = sem("gate_logits_done")
        s_shift = sem("logits_shifted")
        s_exp = sem("gate_exp_done")
        s_route = sem("routing_ready")
        s_wset = sem("weight_set_ready")
        s_pool = sem("pool_step_done")
        s_wbias = sem("weighted_bias_ready")
        s_acc = sem("bias_added")

        block = ctx.enter_context(nc.Block())

        def col(b, t):
            return t * STEP + b * NB

        def down_done(blocks, tiles=0):
            return blocks * KT + tiles

        def down_left(blocks, tiles=0):
            return blocks * KT + (KT * DOWN_BANKS + tiles)

        def slot_order():
            return [(s, t, s * THIRDS + t) for s in range(TOPK) for t in range(THIRDS)]

        def chosen(eng, b):
            return [eng.value_load(top_int[0:1, ds(b, 1), s:s + 1], min_val=0, max_val=E - 1)
                    for s in range(TOPK)]

        def unless_hidden(eng, expert, t, work, skip):
            if t not in HIDDEN_FROM:
                work()
            else:
                with eng.If(expert != HIDDEN_FROM[t]):
                    work()
                with eng.Else():
                    skip()

        @block.sync
        def _(sp):
            sp.dma_start(par[:, :], small).then_inc(s_small, 16)
            sp.dma_start(gbias[:, :], gate_bias.partition_broadcast(P)).then_inc(s_small, 16)

            def load_w2(dst, stage, c):
                r = slice(RANK_CUTS[c], RANK_CUTS[c + 1])
                sp.dma_start(dst[:, r, :, :], w2[stage, :, r, :, :]).then_inc(
                    s_w2[CHUNKS * stage + c], 16)
            def load_x(t):
                n = slice(t * STEP, (t + 1) * STEP)
                sp.dma_start(x[:, :, n], xT[:, :, n]).then_inc(s_x[t], 16)

            def load_base(stage):
                sp.dma_start(base_w[:, stage, :, :], base[:, stage, :, :]).then_inc(s_base[stage], 16)

            for c in range(CHUNKS):
                load_w2(w2_a, 0, c)
                if c == 0:
                    sp.dma_start(b2s[:, :], bias2).then_inc(s_aux, 16)
            load_x(0)
            load_base(0)
            load_w2(w2_b, 1, 0)
            load_x(1)
            for c in range(1, CHUNKS):
                load_w2(w2_b, 1, c)
                if c == 2:
                    load_x(2)
            load_base(1)

            def load_expert(n, src):
                if n:
                    sp.wait_ge(s_wset, 2 * n)
                sp.dma_start(landing[:, 0:BIASC + W1C], src[:, 0:BIASC + W1C]).then_inc(s_w1land, 16)
                sp.dma_start(landing[:, BIASC + W1C:EXPERTC],
                             src[:, BIASC + W1C:EXPERTC]).then_inc(s_w2land, 16)

            load_expert(0, experts[E, :, :])
            sp.wait_ge(s_route, 1)
            for b in range(B):
                for s in range(TOPK):
                    e = sp.value_load(top_int[0:1, b, s:s + 1], min_val=0, max_val=E - 1)
                    load_expert(1 + b * TOPK + s,
                                experts[ds(e, 1), :, :].rearrange("e p n -> (e p) n"))
            for b in range(B):
                for t in range(THIRDS):
                    c = col(b, t)
                    for k in range(KT):
                        sp.wait_ge(s_evac, down_left((2 + b) * BLOCKS + (TOPK - 1) * THIRDS + t, k + 1))
                        sp.dma_start(out[:, k, c:c + NB], x[:, k, c:c + NB]).then_inc(s_out, 16)
            sp.wait_ge(s_out, 16 * BLOCKS * KT)

        @block.gpsimd
        def _(pool):
            nc.gpsimd.memset(ones[:, :], 1.0)
            for e in range(E):
                nc.gpsimd.memset(idx_up[:, e:e + 1], float(e))
                nc.gpsimd.memset(idx_down[:, e:e + 1], float(E - e))
            nc.gpsimd.memset(h_diag[:, :], 0.0).then_inc(s_const, 1)

            def subtract(lo, src, hi, done):
                nc.gpsimd.tensor_tensor(lo, src, hi.bitcast(fp32), ALU.subtract).then_inc(done, 1)

            for m in range(BLOCKS):
                pool.wait_ge(s_xhi, m + 1)
                n = slice(m * NB, (m + 1) * NB)
                subtract(x_lo[:, :, n], x[:, :, n], x_hi[:, :, n], s_xsplit)

            hi_done = [0]

            def split(hi, lo, src, done):
                hi_done[0] += 1
                nc.gpsimd.tensor_scalar(hi, src, 1.0, 0.0, ALU.mult, ALU.add).then_inc(s_pool, 1)
                pool.wait_ge(s_pool, hi_done[0])
                subtract(lo, src, hi, done)

            def split_expert(n, weight_set):
                hi, lo = sets[weight_set]
                pool.wait_ge(s_w1land, 16 * (n + 1))
                nc.gpsimd.tensor_scalar(bias_set[:, weight_set, :], landing[:, 0:BIASC], 1.0, 0.0,
                                        ALU.mult, ALU.add)
                split(hi[:, 0:W1C], lo[:, 0:W1C], landing[:, BIASC:BIASC + W1C], s_wset)
                pool.wait_ge(s_w2land, 16 * (n + 1))
                split(hi[:, W1C:W1C + W2C], lo[:, W1C:W1C + W2C], landing[:, BIASC + W1C:EXPERTC],
                      s_wset)

            split_expert(0, SET_A)
            for b in range(B):
                pool.wait_ge(s_evac, down_left(BLOCKS + b * (BLOCKS + THIRDS)))
                split_expert(1 + b * TOPK, SET_B)
                pool.wait_ge(s_evac, down_left((2 + b) * BLOCKS))
                split_expert(2 + b * TOPK, SET_A)

        @block.scalar
        def _(act):
            act.sem_inc(s_gelu, UP_BANKS)
            act.wait_ge(s_small, 32)
            cond = par[:, C_COND:C_COND + KT * B].rearrange("p (k b) -> p k b", k=KT)
            nc.scalar.activation(silu_c[:, :, :], cond, ACT.Silu).then_inc(s_act_small, 1)
            act.wait_ge(s_dve, 4)
            nc.scalar.activation(rstd[:, :], rstd[:, :], ACT.Sqrt).then_inc(s_act_small, 1)
            act.wait_ge(s_pe_small, 3)
            for k in range(KT):
                last = nc.scalar.activation(hcond[:, k, :], HC_PS[:, k * B:(k + 1) * B], ACT.Gelu,
                                            bias=par[:, C_BIAS1 + k:C_BIAS1 + k + 1])
            last.then_inc(s_act_small, 1)

            def x_hi_half(t):
                act.wait_ge(s_x[t], 16)
                for b in range(B):
                    n = slice(col(b, t), col(b, t) + NB)
                    nc.scalar.activation(x_hi[:, :, n], x[:, :, n], ACT.Identity).then_inc(s_xhi, 1)

            for t in range(THIRDS - 1):
                x_hi_half(t)

            def gelu_tile(k, ht, pair, func, **bias):
                if ht % 2 == 0:
                    act.wait_ge(s_split, pair + 1)
                act.wait_ge(s_up, k + 1)
                nc.scalar.activation(act_out[:, ht % UP_BANKS, :], up_ps[:, ht % UP_BANKS, 0:NB],
                                     func, **bias).then_inc(s_gelu, 1)

            def mid_gelu(i):
                for b in range(B):
                    for lt in range(KT):
                        gelu_tile(i * (B * KT) + (b * KT + lt), b * KT + lt, i * B + b, ACT.Gelu)

            with act.Fori(0, THIRDS - 1) as i:
                mid_gelu(i)
            x_hi_half(THIRDS - 1)
            mid_gelu(THIRDS - 1)
            for b in range(B):
                pair = (THIRDS - 1) * B + b
                act.wait_ge(s_gelu, pair * 2 + (2 + UP_BANKS))
                act.wait_ge(s_hi, pair)
                nc.scalar.activation(mid_hi[:, :, col(b, THIRDS - 1):col(b, THIRDS - 1) + NB],
                                     act_out[:, 2 * b:2 * b + 2, :],
                                     ACT.Identity).then_inc(s_hi, 1)

            nc.scalar.preload_act_table(ACT.Gelu_apprx_tanh)
            with act.Fori(0, THIRDS) as i:
                for b in range(B):
                    act.wait_ge(s_evac, down_left(i * B + (b + 1)))
                    for k in range(KT):
                        c = i * STEP + b * NB
                        last = nc.scalar.activation(
                            x_hi[:, k, ds(c, NB)], x[:, k, ds(c, NB)], ACT.Identity,
                            accum_out=sums[:, ds(i, 1), k, b])
                    last.then_inc(s_x1hi, 1)

            def expert_gelu(n, weight_set):
                for ht in range(HT):
                    gelu_tile(n * HT + (MID_TILES + ht), ht, n * PAIRS + (MID_PAIRS + ht // 2),
                              ACT.Gelu_apprx_tanh, bias=bias_set[:, weight_set, ht:ht + 1])

            for b in range(B):
                expert_gelu(b, SET_A)
            act.wait_ge(s_shift, 1)
            nc.scalar.activation(probs[:, :, :], z[:, :, :], ACT.Exp).then_inc(s_exp, 1)
            nc.scalar.preload_act_table(ACT.Gelu_apprx_tanh)
            with act.Fori(1, THIRDS) as i:
                for b in range(B):
                    expert_gelu(i * B + b, SET_A)

            def skip_gelu():
                act.drain().then_inc(s_gelu, HT)

            act.wait_ge(s_route, 1)
            with act.Fori(0, B) as b:
                picked = chosen(act, b)
                for s, t, m in slot_order():
                    unless_hidden(
                        act, picked[s], t,
                        lambda: expert_gelu(b * BLOCKS + (BLOCKS + m), SET_B if s == 0 else SET_A),
                        skip_gelu)

        @block.vector
        def _(dve):
            dve.sem_inc(s_split, ACT_PAIRS)
            dve.sem_inc(s_evac, KT * DOWN_BANKS)
            dve.sem_inc(s_acc, SCALED)
            done = [0]

            def step(ins):
                done[0] += 1
                ins.then_inc(s_dve, 1)
                dve.wait_ge(s_dve, done[0])

            v = nc.vector
            cond = par[:, C_COND:C_COND + KT * B].rearrange("p (k b) -> p k b", k=KT)

            def over_k(a):
                return a.unsqueeze(1).to_broadcast([P, KT, B])

            dve.wait_ge(s_pe_small, 1)
            step(v.tensor_scalar(red[:, :], SUM_PS, 1.0 / D, None, ALU.mult))
            step(v.tensor_tensor(diff[:, :, :], cond, over_k(red[:, :]), ALU.subtract))
            step(v.tensor_tensor(diff2[:, :, :], diff[:, :, :], diff[:, :, :], ALU.mult))
            dve.wait_ge(s_pe_small, 2)
            step(v.tensor_scalar(rstd[:, :], VAR_PS, 1.0 / D, LN_EPS, ALU.mult, ALU.add))
            dve.wait_ge(s_act_small, 2)
            step(v.reciprocal(rinv[:, :], rstd[:, :]))
            step(v.tensor_tensor(cnorm[:, :, :], diff[:, :, :], over_k(rinv[:, :]), ALU.mult))
            for k in range(KT):
                last = v.tensor_scalar(cnorm[:, k, :], cnorm[:, k, :],
                                       par[:, C_GAMMA + k:C_GAMMA + k + 1],
                                       par[:, C_BETA + k:C_BETA + k + 1], ALU.mult, ALU.add)
            step(last)
            timew = par[:, C_TIMEW:C_TIMEW + KT * 2 * E].rearrange("p (k n) -> p k n", k=KT)
            step(v.tensor_tensor(
                mod_prod[:, :, :, :],
                timew.unsqueeze(1).to_broadcast([P, B, KT, 2 * E]),
                silu_c[:, :, :].rearrange("p k b -> p b k").unsqueeze(3).to_broadcast([P, B, KT, 2 * E]),
                ALU.mult))
            dve.wait_ge(s_act_small, 3)
            dve.wait_ge(s_const, 1)
            diag = (h_diag[:, :].rearrange("p (r q) -> p r q", r=RANK)[:, :, 0:KT * 32]
                    .rearrange("p r (k m n) -> p r k m n", k=KT, n=RANK)[:, :, :, 0:B, 0])
            v.tensor_copy(diag, hcond[:, :, :].unsqueeze(1)
                          .to_broadcast([P, RANK, KT, B])).then_inc(s_diag, 1)
            dve.wait_ge(s_pe_small, 4)
            step(v.tensor_tensor(mod[:, :, :], MOD_PS.rearrange("p (b n) -> p b n", b=B),
                                 gbias[:, E:3 * E].unsqueeze(1).to_broadcast([P, B, 2 * E]), ALU.add))
            step(v.tensor_scalar(mod[:, :, 0:E], mod[:, :, 0:E], 1.0, None, ALU.add))

            def factors(stage):
                dve.wait_ge(s_lr, stage + 1)
                step(v.tensor_tensor(lr_half[:, :], LR_PS[64:128, :],
                                     b2s[:, stage * D:(stage + 1) * D], ALU.add))
                step(v.tensor_tensor(lr[:, stage, :], LR_PS[0:64, :], lr_half[:, :], ALU.add))
                v.tensor_tensor(lr_left[32:64, stage, :, :],
                                lr[0:32, stage, :].unsqueeze(1).to_broadcast([32, B, D]),
                                b2s[0:32, 2 * D:2 * D + B].unsqueeze(2).to_broadcast([32, B, D]),
                                ALU.mult).then_inc(s_lr_ready, 1)

            def effective(stage):
                dve.wait_ge(s_base[stage], 16)
                for b in range(B):
                    dve.wait_ge(s_effps, stage * B + b + 1)
                    step(v.tensor_tensor(eff[:, b, :, :],
                                         EFF_PS[b].rearrange("p (k n) -> p k n", k=KT),
                                         base_w[:, stage, :, :], ALU.add))
                    step(v.tensor_copy(eff_hi[stage][:, b, :, :], eff[:, b, :, :]))
                    v.tensor_tensor(eff_lo[stage][:, b, :, :], eff[:, b, :, :],
                                    eff_hi[stage][:, b, :, :].bitcast(fp32),
                                    ALU.subtract).then_inc(s_eff, 1)

            dve.wait_ge(s_aux, 16)
            factors(0)
            effective(0)

            def split_pair(pair, place, hi, lo, hi_by_act=False):
                src = act_out[:, 2 * place:2 * place + 2, :]
                if not hi_by_act:
                    dve.wait_ge(s_gelu, pair * 2 + (2 + UP_BANKS))
                    v.tensor_copy(hi, src).then_inc(s_hi, 1)
                dve.wait_ge(s_hi, pair + 1)
                v.tensor_tensor(lo, src, hi.bitcast(fp32), ALU.subtract).then_inc(s_split, 1)

            def mid_split(i, b, hi_by_act=False):
                c = i * STEP + b * NB
                split_pair(i * B + b, b, mid_hi[:, :, ds(c, NB)], mid_lo[:, :, ds(c, NB)],
                           hi_by_act)

            with dve.Fori(0, THIRDS - 1) as i:
                for b in range(B):
                    mid_split(i, b)
            factors(1)
            effective(1)
            def result(i, batches=range(B)):
                for b in batches:
                    c = i * STEP + b * NB
                    dve.wait_ge(s_down, down_done(i * B + (b + 1)))
                    v.scalar_tensor_tensor(x[:, :, ds(c, NB)], x[:, :, ds(c, NB)], 2.0,
                                           down_ps[:, b, :, 0:NB], ALU.mult,
                                           ALU.add).then_inc(s_evac, KT)

            def result_lo(i):
                for b in range(B):
                    c = i * STEP + b * NB
                    dve.wait_ge(s_x1hi, i * B + (b + 1))
                    v.tensor_tensor(x_lo[:, :, ds(c, NB)], x[:, :, ds(c, NB)],
                                    x_hi[:, :, ds(c, NB)].bitcast(fp32),
                                    ALU.subtract).then_inc(s_x1lo, 1)

            mid_split(THIRDS - 1, 0, hi_by_act=True)
            result(0, [0])
            mid_split(THIRDS - 1, 1, hi_by_act=True)
            result(0, [1])
            result_lo(0)
            with dve.Fori(1, THIRDS) as i:
                result(i)
                result_lo(i)

            x5 = x[:, :, :].rearrange("p k (t b n) -> p t k b n", b=B, t=THIRDS)
            step(v.tensor_tensor(sums[:, 0:2, :, :], sums[:, 0:2, :, :], x5[:, 0:2, :, :, NB - 1],
                                 ALU.subtract))
            head, wrist, proprio = (sums[:, t, :, :] for t in range(THIRDS))
            v.tensor_tensor(aggs[:, 2, :, :], wrist, proprio, ALU.add)
            step(v.tensor_tensor(aggs[:, 1, :, :], head, proprio, ALU.add))
            step(v.tensor_tensor(aggs[:, 0, :, :], aggs[:, 1, :, :], wrist, ALU.add))
            v.tensor_scalar(aggs[:, 0, :, :], aggs[:, 0, :, :], 1.0 / T, None, ALU.mult)
            step(v.tensor_scalar(aggs[:, 1:3, :, :], aggs[:, 1:3, :, :], 1.0 / (T - THIRD), None,
                                 ALU.mult))
            gatew = par[:, C_GATEW:C_GATEW + THIRDS * KT * E].rearrange("p (c e) -> p c e", e=E)
            full = [P, B, THIRDS * KT, E]
            v.tensor_tensor(gate_prod[:, :, :, :], gatew.unsqueeze(1).to_broadcast(full),
                            aggs[:, :, :, :].rearrange("p g k b -> p b (g k)").unsqueeze(3)
                            .to_broadcast(full), ALU.mult).then_inc(s_gprod, 1)

            def over_e(a):
                return a.unsqueeze(2).to_broadcast([P, B, E])

            def over_b(a):
                return a.unsqueeze(1).to_broadcast([P, B, E])

            def route_logits():
                dve.wait_ge(s_gate, 1)
                step(v.tensor_tensor(z[:, :, :], GATE_PS.rearrange("p (b e) -> p b e", b=B),
                                     over_b(gbias[:, 0:E]), ALU.add))
                step(v.tensor_tensor(z[:, :, :], z[:, :, :], mod[:, :, 0:E], ALU.mult))
                step(v.tensor_tensor(z[:, :, :], z[:, :, :], mod[:, :, E:2 * E], ALU.add))
                step(v.tensor_reduce(red[:, :], z[:, :, :], AX.X, ALU.max))
                v.tensor_tensor(z[:, :, :], z[:, :, :], over_e(red[:, :]),
                                ALU.subtract).then_inc(s_shift, 1)

            def route_topk():
                dve.wait_ge(s_exp, 1)
                step(v.tensor_reduce(red[:, :], probs[:, :, :], AX.X, ALU.add))
                step(v.reciprocal(rinv[:, :], red[:, :]))
                step(v.tensor_tensor(probs[:, :, :], probs[:, :, :], over_e(rinv[:, :]), ALU.mult))
                for s in range(TOPK):
                    step(v.tensor_reduce(top_v[:, :, s], probs[:, :, :], AX.X, ALU.max))
                    step(v.tensor_tensor(eqt[:, :, :], probs[:, :, :], over_e(top_v[:, :, s]),
                                         ALU.is_equal))
                    step(v.tensor_tensor(eqt[:, :, :], eqt[:, :, :], over_b(idx_down[:, :]), ALU.mult))
                    step(v.tensor_reduce(red[:, :], eqt[:, :, :], AX.X, ALU.max))
                    step(v.tensor_scalar(top_i[:, :, s], red[:, :], -1.0, float(E), ALU.mult, ALU.add))
                    if s == 0:
                        step(v.tensor_tensor(eqt[:, :, :], over_b(idx_up[:, :]),
                                             over_e(top_i[:, :, s]), ALU.is_equal))
                        step(v.scalar_tensor_tensor(probs[:, :, :], eqt[:, :, :], -2.0,
                                                    probs[:, :, :], ALU.mult, ALU.add))
                v.tensor_copy(top_int[:, :, :], top_i[:, :, :]).then_inc(s_route, 1)
                step(v.tensor_tensor(red[:, :], top_v[:, :, 0], top_v[:, :, 1], ALU.add))
                step(v.tensor_scalar(red[:, :], red[:, :], 1e-8, None, ALU.add))
                step(v.reciprocal(rinv[:, :], red[:, :]))
                step(v.tensor_tensor(weights[:, :].rearrange("p (b s) -> p b s", b=B),
                                     top_v[:, :, :],
                                     rinv[:, :].unsqueeze(2).to_broadcast([P, B, TOPK]), ALU.mult))

            def expert_splits(n, parity):
                dve.wait_ge(s_down, down_done(n + (BLOCKS - 1)))
                for q in range(PAIRS):
                    split_pair(n * PAIRS + (MID_PAIRS + q), q % 2,
                               h_hi[:, parity, 2 * q:2 * q + 2, :], h_lo[:, parity, 2 * q:2 * q + 2, :])

            def add_shared(n, b, c):
                for k in range(KT):
                    dve.wait_ge(s_down, down_done(n + BLOCKS, k + 1))
                    v.scalar_tensor_tensor(
                        x[:, k, ds(c, NB)], down_ps[:, b, k, 0:NB],
                        bias_set[:, SET_A, HT + k:HT + k + 1], x[:, k, ds(c, NB)], ALU.add,
                        ALU.add).then_inc(s_evac, 1)

            def add_expert(n, done_before, parity, weight_set, w_at, c):
                weight = weights[:, ds(w_at, 1)]
                dve.wait_ge(s_acc, done_before + SCALED)
                v.tensor_scalar(wbias[:, :], bias_set[:, weight_set, HT:HT + KT], weight, None,
                                ALU.mult).then_inc(s_wbias, 1)
                dve.wait_ge(s_wbias, done_before + 1)
                for k in range(KT):
                    last = v.tensor_scalar(x[:, k, ds(c, NB)], x[:, k, ds(c, NB)], wbias[:, k:k + 1],
                                           None, ALU.add)
                last.then_inc(s_acc, 1)
                dve.wait_ge(s_acc, done_before + 1 + SCALED)
                for k in range(KT):
                    dve.wait_ge(s_down, down_done(n + BLOCKS, k + 1))
                    v.scalar_tensor_tensor(
                        x[:, k, ds(c, NB)], down_ps[:, parity, k, 0:NB], weight,
                        x[:, k, ds(c, NB)], ALU.mult, ALU.add).then_inc(s_evac, 1)

            expert_splits(0, 0)
            route_logits()
            expert_splits(1, 1)
            route_topk()
            for b in range(B):
                add_shared(b, b, col(b, 0))
            with dve.Fori(1, THIRDS) as i:
                for b in range(B):
                    expert_splits(i * B + b, b)
                for b in range(B):
                    add_shared(i * B + b, b, i * STEP + b * NB)

            def skip_splits():
                dve.drain().then_inc(s_hi, PAIRS)
                dve.drain().then_inc(s_split, PAIRS)

            def skip_add():
                dve.drain().then_inc(s_wbias, 1)
                dve.drain().then_inc(s_acc, 1)
                dve.drain().then_inc(s_evac, KT)

            dve.wait_ge(s_route, 1)
            with dve.Fori(0, B) as b:
                picked = chosen(dve, b)
                order = slot_order()
                for m in range(BLOCKS + 1):
                    if m < BLOCKS:
                        s, t, _ = order[m]
                        unless_hidden(
                            dve, picked[s], t,
                            lambda: expert_splits(b * BLOCKS + (BLOCKS + m), m % 2), skip_splits)
                    if m:
                        s, t, last = order[m - 1]
                        unless_hidden(
                            dve, picked[s], t,
                            lambda: add_expert(b * BLOCKS + (BLOCKS + last), b * BLOCKS + last,
                                               last % 2, SET_B if s == 0 else SET_A,
                                               b * TOPK + s, b * NB + t * STEP), skip_add)

        @block.tensor
        def _(pe):
            mm = nc.tensor.matmul

            def product(dst, w_hi, w_lo, v_hi, v_lo, start, stop):
                mm(dst, w_lo, v_hi, start=start, stop=False)
                mm(dst, w_hi, v_hi, start=False, stop=False)
                return mm(dst, w_hi, v_lo, start=False, stop=stop)

            pe.wait_ge(s_small, 32)
            pe.wait_ge(s_const, 1)
            cond = par[:, C_COND:C_COND + KT * B].rearrange("p (k b) -> p k b", k=KT)
            for k in range(KT):
                last = mm(SUM_PS, ones[:, :], cond[:, k, :], start=k == 0, stop=k == KT - 1)
            last.then_inc(s_pe_small, 1)
            pe.wait_ge(s_dve, 3)
            for k in range(KT):
                last = mm(VAR_PS, ones[:, :], diff2[:, k, :], start=k == 0, stop=k == KT - 1)
            last.then_inc(s_pe_small, 1)
            pe.wait_ge(s_dve, 7)
            for n in range(KT):
                for k in range(KT):
                    at = C_W1 + k * D + n * P
                    last = mm(HC_PS[:, n * B:(n + 1) * B], par[:, at:at + P], cnorm[:, k, :],
                              start=k == 0, stop=k == KT - 1)
            last.then_inc(s_pe_small, 1)
            pe.wait_ge(s_dve, 8)
            for k in range(KT):
                last = mm(MOD_PS, ones[:, :], mod_prod[:, :, k, :], start=k == 0, stop=k == KT - 1)
            last.then_inc(s_pe_small, 1)

            def low_rank(stage, w2_sb, chunks):
                for c in chunks:
                    pe.wait_ge(s_w2[CHUNKS * stage + c], 16)
                    for r in range(RANK_CUTS[c], RANK_CUTS[c + 1]):
                        for k in range(KT):
                            for side in range(2):
                                at = r * KT * 32 + k * 32
                                row = 32 * (2 * k + side)
                                last = mm(LR_PS[row:row + 32, :], h_diag[:, at:at + 32],
                                          w2_sb[:, r, k, side * D:(side + 1) * D],
                                          start=r == 0, stop=r == RANK - 1)
                if c == CHUNKS - 1:
                    last.then_inc(s_lr, 1)

            def fold(stage):
                pe.wait_ge(s_lr_ready, stage + 1)
                for b in range(B):
                    for k in range(KT):
                        last = mm(EFF_PS[b][:, k * D:(k + 1) * D],
                                  lr_left[32:64, stage, b, k * P:(k + 1) * P],
                                  lr[32:64, stage, :], start=True, stop=True)
                    last.then_inc(s_effps, 1)

            pe.wait_ge(s_diag, 1)
            low_rank(0, w2_a, range(CHUNKS))
            fold(0)
            low_rank(1, w2_b, range(1))

            def mid_product(i, b):
                c = i * STEP + b * NB
                pe.wait_ge(s_eff, b + 1)
                pe.wait_ge(s_xsplit, i * B + (b + 1))
                for lt in range(KT):
                    pe.wait_ge(s_gelu, i * (B * KT) + (b * KT + lt + 1))
                    for k in range(KT):
                        n = slice(lt * P, (lt + 1) * P)
                        last = product(up_ps[:, b * KT + lt, 0:NB], eff_hi[0][:, b, k, n],
                                       eff_lo[0][:, b, k, n], x_hi[:, k, ds(c, NB)],
                                       x_lo[:, k, ds(c, NB)], k == 0, k == KT - 1)
                    last.then_inc(s_up, 1)

            with pe.Fori(0, THIRDS - 1) as i:
                for b in range(B):
                    mid_product(i, b)
            low_rank(1, w2_b, range(1, CHUNKS))
            mid_product(THIRDS - 1, 0)
            fold(1)
            mid_product(THIRDS - 1, 1)

            with pe.Fori(0, THIRDS) as i:
                for b in range(B):
                    c = i * STEP + b * NB
                    pe.wait_ge(s_eff, B + b + 1)
                    pe.wait_ge(s_split, i * B + (b + 1 + ACT_PAIRS))
                    pe.wait_ge(s_evac, down_left(i * B + (b + 1 - DOWN_BANKS)))
                    for dt in range(KT):
                        for k in range(KT):
                            n = slice(dt * P, (dt + 1) * P)
                            last = product(down_ps[:, b, dt, 0:NB], eff_hi[1][:, b, k, n],
                                           eff_lo[1][:, b, k, n], mid_hi[:, k, ds(c, NB)],
                                           mid_lo[:, k, ds(c, NB)], k == 0, k == KT - 1)
                        last.then_inc(s_down, 1)

            def expert_up(n, weight_set, c):
                hi, lo = sets[weight_set]
                for ht in range(HT):
                    pe.wait_ge(s_gelu, n * HT + (MID_TILES + ht + 1))
                    for k in range(KT):
                        at = k * H + ht * P
                        last = product(up_ps[:, ht % UP_BANKS, 0:NB], hi[:, at:at + P],
                                       lo[:, at:at + P], x_hi[:, k, ds(c, NB)],
                                       x_lo[:, k, ds(c, NB)], k == 0, k == KT - 1)
                    last.then_inc(s_up, 1)

            def expert_down(n, parity, weight_set):
                hi, lo = sets[weight_set]
                pe.wait_ge(s_evac, down_left(n + (BLOCKS + 1 - DOWN_BANKS)))
                for q in range(PAIRS):
                    pe.wait_ge(s_split, n * PAIRS + (MID_PAIRS + q + 1 + ACT_PAIRS))
                    for dt in range(KT):
                        for ht in (2 * q, 2 * q + 1):
                            at = W1C + ht * D + dt * P
                            last = product(down_ps[:, parity, dt, 0:NB], hi[:, at:at + P],
                                           lo[:, at:at + P], h_hi[:, parity, ht, :],
                                           h_lo[:, parity, ht, :], ht == 0, ht == HT - 1)
                        if q == PAIRS - 1:
                            last.then_inc(s_down, 1)

            pe.wait_ge(s_wset, 1)
            for b in range(B):
                pe.wait_ge(s_x1lo, b + 1)
                expert_up(b, SET_A, col(b, 0))
                if b == 0:
                    pe.wait_ge(s_gprod, 1)
                    pe.wait_ge(s_evac, down_left(BLOCKS))
                    for g in range(THIRDS * KT):
                        last = mm(GATE_PS, ones[:, :], gate_prod[:, :, g, :], start=g == 0,
                                  stop=g == THIRDS * KT - 1)
                    last.then_inc(s_gate, 1)
            pe.wait_ge(s_wset, 2)
            pe.wait_ge(s_shift, 1)
            for b in range(B):
                expert_down(b, b, SET_A)
            with pe.Fori(1, THIRDS) as i:
                for b in range(B):
                    pe.wait_ge(s_x1lo, i * B + (b + 1))
                    expert_up(i * B + b, SET_A, i * STEP + b * NB)
                for b in range(B):
                    expert_down(i * B + b, b, SET_A)

            def skip_up():
                pe.drain().then_inc(s_up, HT)

            def skip_down():
                pe.drain().then_inc(s_down, KT)

            pe.wait_ge(s_route, 1)
            with pe.Fori(0, B) as b:
                picked = chosen(pe, b)
                order = slot_order()
                for m in range(BLOCKS + 1):
                    if m < BLOCKS:
                        s, t, _ = order[m]
                        if t == 0:
                            pe.wait_ge(s_wset, b * (2 * TOPK) + (3 + 2 * s))
                        unless_hidden(
                            pe, picked[s], t,
                            lambda: expert_up(b * BLOCKS + (BLOCKS + m), SET_B if s == 0 else SET_A,
                                              b * NB + t * STEP), skip_up)
                    if m:
                        s, t, last = order[m - 1]
                        if t == 0:
                            pe.wait_ge(s_wset, b * (2 * TOPK) + (4 + 2 * s))
                        unless_hidden(
                            pe, picked[s], t,
                            lambda: expert_down(b * BLOCKS + (BLOCKS + last), last % 2,
                                                SET_B if s == 0 else SET_A), skip_down)


def kernel(**inputs):
    import numpy as np
    import concourse.bacc as bacc
    from concourse.bass_utils import run_bass_kernel_spmd as run

    a = {k: np.asarray(v) for k, v in inputs.items()}

    def rows(w):
        return w.reshape(-1, P, w.shape[-1]).transpose(1, 0, 2).reshape(P, -1)

    def vec(v):
        return v.reshape(-1, P).T

    cuts = [slice(t * THIRD, t * THIRD + NB) for t in range(THIRDS)]
    xp = np.stack([a["x"][:, c] for c in cuts])
    xT = xp.reshape(COLS, KT, P).transpose(2, 1, 0)
    small = np.concatenate([
        rows(a["cond_1024"].T), vec(a["L0_cond_ln_gamma"]), vec(a["L0_cond_ln_beta"]),
        vec(a["L0_cond_bias1"]), rows(a["L1_cond_time_w"]), rows(a["L1_cond_gate_w"]),
        rows(a["L0_cond_W1"])], axis=1)
    gate_bias = np.concatenate([a["L1_cond_gate_b"], a["L1_cond_time_b"]])
    parts = [2, 3, 1, 0]
    w2 = a["L0_cond_W2"].reshape(KT, P, 4, D, RANK)[:, :, parts]
    w2 = w2.reshape(KT, P, 2, 2, D, RANK).transpose(2, 1, 5, 0, 3, 4).reshape(2, P, RANK, KT, 2 * D)
    b2 = a["L0_cond_bias2"].reshape(4, D, RANK)[parts].reshape(2, 2 * D, RANK).transpose(2, 0, 1)
    bias2 = np.zeros((2, 32, 2 * D + B), np.float32)
    for b in range(B):
        bias2[:, b * RANK:(b + 1) * RANK, 0:2 * D] = (
            b2.reshape(RANK, 2, 2, D).transpose(2, 0, 1, 3).reshape(2, RANK, 2 * D))
        bias2[:, b * RANK:(b + 1) * RANK, 2 * D + b] = 1
    bias2 = bias2.reshape(64, 2 * D + B)
    base = np.stack([rows(a["L0_cond_base_down"]).reshape(P, KT, D),
                     rows(a["L0_cond_base_up"].T).reshape(P, KT, D)], axis=1)

    def expert(w1, b1, w2_, b2_):
        return np.concatenate([vec(b1), vec(b2_), rows(w1), rows(w2_)], axis=1)

    experts = np.stack(
        [expert(a["L1_cond_ew1"][e], a["L1_cond_eb1"][e], a["L1_cond_ew2"][e], a["L1_cond_eb2"][e])
         for e in range(E)]
        + [expert(a["L1_cond_sw1"], a["L1_cond_sb1"], a["L1_cond_sw2"], a["L1_cond_sb2"])])

    nc = bacc.Bacc("TRN2", target_bir_lowering=False, num_devices=1)
    arrays, aps = {}, []
    for name, value in (("xT", xT), ("small", small), ("gate_bias", gate_bias), ("w2", w2),
                        ("bias2", bias2), ("base", base), ("experts", experts)):
        arrays[name] = np.ascontiguousarray(value)
        aps.append(nc.dram_tensor(name, arrays[name].shape, mybir.dt.float32,
                                  kind="ExternalInput").ap())
    aps.append(nc.dram_tensor("yT", (P, KT, COLS), mybir.dt.float32, kind="ExternalOutput").ap())
    build(nc, *aps)
    y = run(nc, [arrays], core_ids=[0]).results[0]["yT"]
    y = y.transpose(2, 1, 0).reshape(THIRDS, B, NB, D)
    return np.concatenate([y[0, :, 0:THIRD], y[1, :, 0:THIRD], y[2]], axis=1)
```
